# Optimizing a Trainium2 kernel written in Bass

```python
import numpy as np
import jax
import jax.numpy as jnp

def _softmax(x, axis=-1):
    return jax.nn.softmax(x, axis=axis)

def _gelu(x):
    return jax.nn.gelu(x, approximate=True)

def _silu(x):
    return jax.nn.silu(x)

def _sigmoid(x):
    return jax.nn.sigmoid(x)

def _layernorm(x, axis=-1, eps=1e-05):
    m = jnp.mean(x, axis=axis, keepdims=True)
    v = jnp.var(x, axis=axis, keepdims=True)
    return (x - m) / jnp.sqrt(v + eps)

def _scatter_add(tgt, idx, src, axis=0):
    return tgt.at[idx].add(src)

def _segment_sum(src, seg, n):
    return jax.ops.segment_sum(src, seg, n)
kernel_name = 'mk_perceiver_d1_seqx_r2_f9c0ec'

def setup_inputs(seed: int=0):
    np.random.seed(seed)
    _w = jnp.asarray

    def _rec_inputs():
        import jax
        import jax.numpy as jnp
        _rk = jax.random.key(seed)
        x = 7.22e-05 + 1 * jax.random.normal(jax.random.fold_in(_rk, 1), (2, 128, 512), jnp.float32)
        _lenS = 128 - jax.random.randint(jax.random.fold_in(_rk, 7), (2,), 0, max(1, 128 // 4) + 1, jnp.int32)
        _lenS2 = 2048 - jax.random.randint(jax.random.fold_in(_rk, 8), (2,), 0, max(1, 2048 // 4) + 1, jnp.int32)
        _ctx_1024P = jax.random.normal(jax.random.fold_in(_rk, 11), (2, 16, 512), jnp.float32)
        _ctx_1024c = jax.random.dirichlet(jax.random.fold_in(_rk, 511), 0.3 * jnp.ones((16,), jnp.float32), (2, 2048))
        _ctx_1024t = jnp.einsum('bsk,bkd->bsd', _ctx_1024c, _ctx_1024P)
        _ctx_1024t = _ctx_1024t * jax.lax.rsqrt(jnp.mean(jnp.square(_ctx_1024t)) + 1e-12) * 0.953939
        ctx_1024 = 4.13588e-05 + 0.999923 * (_ctx_1024t + 0.3 * jax.random.normal(jax.random.fold_in(_rk, 611), (2, 2048, 512), jnp.float32))
        _validS = jnp.arange(128)[None, :] < _lenS[:, None]
        _validS2 = jnp.arange(2048)[None, :] < _lenS2[:, None]
        _causal = jnp.tril(jnp.ones((128, 128), dtype=bool))
        mask_BxS2_bf0 = jnp.logical_not(jnp.ones((2, 2048), dtype=bool))
        return (x, ctx_1024, mask_BxS2_bf0)
    x, ctx_1024, mask_BxS2_bf0 = _rec_inputs()

    def _L0_xattn_setup():
        import jax, jax.numpy as jnp
        import numpy as np
        N_HEADS = 16
        DIM = 512
        HEAD_DIM = DIM // N_HEADS

        def _split_heads(t):
            B, S, _ = t.shape
            return t.reshape(B, S, N_HEADS, HEAD_DIM).transpose(0, 2, 1, 3)
        key = jax.random.key(seed)
        ks = jax.random.split(key, 12)
        B, S = (4, 1024)
        scale = 1.0 / np.sqrt(DIM)
        inp = {'x': jax.random.normal(ks[0], (B, S, DIM), jnp.float32), 'memory': jax.random.normal(ks[1], (B, S, DIM), jnp.float32), 'mask': jnp.zeros((B, S), jnp.bool_), 'wq': jax.random.normal(ks[2], (DIM, DIM), jnp.float32) * scale, 'bq': jnp.zeros((DIM,), jnp.float32), 'wk': jax.random.normal(ks[3], (DIM, DIM), jnp.float32) * scale, 'bk': jnp.zeros((DIM,), jnp.float32), 'wv': jax.random.normal(ks[4], (DIM, DIM), jnp.float32) * scale, 'bv': jnp.zeros((DIM,), jnp.float32), 'wo': jax.random.normal(ks[5], (DIM, DIM), jnp.float32) * scale, 'bo': jnp.zeros((DIM,), jnp.float32)}
        return inp
    _L0_xattn_all = _L0_xattn_setup()
    _L0_xattn_in = {k: v for k, v in _L0_xattn_all.items() if k in ('wq', 'bq', 'wk', 'bk', 'wv', 'bv', 'wo', 'bo')}
    del _L0_xattn_all

    def _L0_attn_setup():
        import jax, jax.numpy as jnp
        import numpy as np
        import math
        B, T, D = (2, 2048, 512)
        H = 16
        HEAD_DIM = D // H
        CHUNK = 64

        def chunked_attention(q, k, v, chunk_size, scale):
            Bq, Hq, Tq, hd = q.shape
            S = k.shape[2]
            nc = Tq // chunk_size
            q_chunks = q.reshape(Bq, Hq, nc, chunk_size, hd).transpose(2, 0, 1, 3, 4)
            starts = jnp.arange(nc, dtype=jnp.int32) * chunk_size
            k_pos = jnp.arange(S)

            def body(carry, xs):
                qc, start = xs
                scores = jnp.einsum('bhqd,bhkd->bhqk', qc, k) * scale
                q_pos = start + jnp.arange(chunk_size)
                causal_mask = k_pos[None, :] > q_pos[:, None]
                scores = jnp.where(causal_mask[None, None], -jnp.inf, scores)
                m = jnp.max(scores, axis=-1, keepdims=True)
                m = jnp.where(jnp.isinf(m), jnp.zeros_like(m), m)
                p = jax.nn.softmax(scores - m, axis=-1)
                oc = jnp.einsum('bhqk,bhkd->bhqd', p, v)
                return (carry, oc)
            _, outs = jax.lax.scan(body, None, (q_chunks, starts))
            return outs.transpose(1, 2, 0, 3, 4).reshape(Bq, Hq, Tq, hd)
        key = jax.random.key(seed)
        ks = jax.random.split(key, 9)
        s = 1.0 / math.sqrt(D)
        return {'x': jax.random.normal(ks[0], (B, T, D), dtype=jnp.float32), 'Wq': jax.random.normal(ks[1], (D, D), dtype=jnp.float32) * s, 'bq': jax.random.normal(ks[2], (D,), dtype=jnp.float32) * 0.01, 'Wk': jax.random.normal(ks[3], (D, D), dtype=jnp.float32) * s, 'bk': jax.random.normal(ks[4], (D,), dtype=jnp.float32) * 0.01, 'Wv': jax.random.normal(ks[5], (D, D), dtype=jnp.float32) * s, 'bv': jax.random.normal(ks[6], (D,), dtype=jnp.float32) * 0.01, 'Wo': jax.random.normal(ks[7], (D, D), dtype=jnp.float32) * s, 'bo': jax.random.normal(ks[8], (D,), dtype=jnp.float32) * 0.01}
    _L0_attn_all = _L0_attn_setup()
    _L0_attn_in = {k: v for k, v in _L0_attn_all.items() if k in ('Wq', 'bq', 'Wk', 'bk', 'Wv', 'bv', 'Wo', 'bo')}
    del _L0_attn_all

    def _L0_ffn_setup():
        import jax, jax.numpy as jnp
        import numpy as np
        from jax import lax
        D_MODEL = 512
        INTER = 512
        N_EXPERTS = 8
        TOP_K = 2
        ROUTE_SCALE = 1.0
        B, S = (2, 2048)
        key = jax.random.key(seed)
        ks = jax.random.split(key, 16)
        sc_d = 1.0 / np.sqrt(D_MODEL)
        sc_f = 1.0 / np.sqrt(INTER)
        inp = {'x': jax.random.normal(ks[0], (B, S, D_MODEL), dtype=jnp.float32), 'gate_w': jax.random.normal(ks[1], (N_EXPERTS, D_MODEL), dtype=jnp.float32) * sc_d, 'w1': jax.random.normal(ks[2], (N_EXPERTS, D_MODEL, INTER), dtype=jnp.float32) * sc_d, 'b1': jnp.zeros((N_EXPERTS, INTER), dtype=jnp.float32), 'w2': jax.random.normal(ks[3], (N_EXPERTS, INTER, D_MODEL), dtype=jnp.float32) * sc_f, 'b2': jnp.zeros((N_EXPERTS, D_MODEL), dtype=jnp.float32), 'w3': jax.random.normal(ks[4], (N_EXPERTS, D_MODEL, INTER), dtype=jnp.float32) * sc_d, 'b3': jnp.zeros((N_EXPERTS, INTER), dtype=jnp.float32), 'sw1': jax.random.normal(ks[5], (D_MODEL, INTER), dtype=jnp.float32) * sc_d, 'sb1': jnp.zeros((INTER,), dtype=jnp.float32), 'sw2': jax.random.normal(ks[6], (INTER, D_MODEL), dtype=jnp.float32) * sc_f, 'sb2': jnp.zeros((D_MODEL,), dtype=jnp.float32), 'sw3': jax.random.normal(ks[7], (D_MODEL, INTER), dtype=jnp.float32) * sc_d, 'sb3': jnp.zeros((INTER,), dtype=jnp.float32)}
        return inp
    _L0_ffn_all = _L0_ffn_setup()
    _L0_ffn_in = {k: v for k, v in _L0_ffn_all.items() if k in ('gate_w', 'w1', 'b1', 'w2', 'b2', 'w3', 'b3', 'sw1', 'sb1', 'sw2', 'sb2', 'sw3', 'sb3')}
    del _L0_ffn_all
    return {'x': x, 'ctx_1024': ctx_1024, 'mask_BxS2_bf0': mask_BxS2_bf0, 'L0_xattn_wq': _L0_xattn_in['wq'], 'L0_xattn_bq': _L0_xattn_in['bq'], 'L0_xattn_wk': _L0_xattn_in['wk'], 'L0_xattn_bk': _L0_xattn_in['bk'], 'L0_xattn_wv': _L0_xattn_in['wv'], 'L0_xattn_bv': _L0_xattn_in['bv'], 'L0_xattn_wo': _L0_xattn_in['wo'], 'L0_xattn_bo': _L0_xattn_in['bo'], 'L0_attn_Wq': _L0_attn_in['Wq'], 'L0_attn_bq': _L0_attn_in['bq'], 'L0_attn_Wk': _L0_attn_in['Wk'], 'L0_attn_bk': _L0_attn_in['bk'], 'L0_attn_Wv': _L0_attn_in['Wv'], 'L0_attn_bv': _L0_attn_in['bv'], 'L0_attn_Wo': _L0_attn_in['Wo'], 'L0_attn_bo': _L0_attn_in['bo'], 'L0_ffn_gate_w': _L0_ffn_in['gate_w'], 'L0_ffn_w1': _L0_ffn_in['w1'], 'L0_ffn_b1': _L0_ffn_in['b1'], 'L0_ffn_w2': _L0_ffn_in['w2'], 'L0_ffn_b2': _L0_ffn_in['b2'], 'L0_ffn_w3': _L0_ffn_in['w3'], 'L0_ffn_b3': _L0_ffn_in['b3'], 'L0_ffn_sw1': _L0_ffn_in['sw1'], 'L0_ffn_sb1': _L0_ffn_in['sb1'], 'L0_ffn_sw2': _L0_ffn_in['sw2'], 'L0_ffn_sb2': _L0_ffn_in['sb2'], 'L0_ffn_sw3': _L0_ffn_in['sw3'], 'L0_ffn_sb3': _L0_ffn_in['sb3']}

def reference(x, ctx_1024, mask_BxS2_bf0, L0_xattn_wq, L0_xattn_bq, L0_xattn_wk, L0_xattn_bk, L0_xattn_wv, L0_xattn_bv, L0_xattn_wo, L0_xattn_bo, L0_attn_Wq, L0_attn_bq, L0_attn_Wk, L0_attn_bk, L0_attn_Wv, L0_attn_bv, L0_attn_Wo, L0_attn_bo, L0_ffn_gate_w, L0_ffn_w1, L0_ffn_b1, L0_ffn_w2, L0_ffn_b2, L0_ffn_w3, L0_ffn_b3, L0_ffn_sw1, L0_ffn_sb1, L0_ffn_sw2, L0_ffn_sb2, L0_ffn_sw3, L0_ffn_sb3):
    import jax
    import jax.numpy as jnp

    def _L0_xattn_ref(x, memory, mask, wq, bq, wk, bk, wv, bv, wo, bo):
        import jax, jax.numpy as jnp
        import numpy as np
        N_HEADS = 16
        DIM = 512
        HEAD_DIM = DIM // N_HEADS

        def _split_heads(t):
            B, S, _ = t.shape
            return t.reshape(B, S, N_HEADS, HEAD_DIM).transpose(0, 2, 1, 3)
        B, Sq, _ = x.shape
        q = _split_heads(x @ wq.T + bq) / np.sqrt(HEAD_DIM)
        k = _split_heads(memory @ wk.T + bk)
        v = _split_heads(memory @ wv.T + bv)
        logit = jnp.einsum('bhqd,bhkd->bhqk', q, k)
        m = mask[:, None, None, :]
        logit = jnp.where(m, -jnp.inf, logit)
        weights = jax.nn.softmax(logit, axis=-1)
        out = jnp.einsum('bhqk,bhkd->bhqd', weights, v)
        out = out.transpose(0, 2, 1, 3).reshape(B, Sq, DIM)
        return out @ wo.T + bo

    def _L0_attn_ref(x, Wq, bq, Wk, bk, Wv, bv, Wo, bo):
        import jax, jax.numpy as jnp
        import numpy as np
        import math
        B, T, D = (2, 2048, 512)
        H = 16
        HEAD_DIM = D // H
        CHUNK = 64

        def chunked_attention(q, k, v, chunk_size, scale):
            Bq, Hq, Tq, hd = q.shape
            S = k.shape[2]
            nc = Tq // chunk_size
            q_chunks = q.reshape(Bq, Hq, nc, chunk_size, hd).transpose(2, 0, 1, 3, 4)
            starts = jnp.arange(nc, dtype=jnp.int32) * chunk_size
            k_pos = jnp.arange(S)

            def body(carry, xs):
                qc, start = xs
                scores = jnp.einsum('bhqd,bhkd->bhqk', qc, k) * scale
                q_pos = start + jnp.arange(chunk_size)
                causal_mask = k_pos[None, :] > q_pos[:, None]
                scores = jnp.where(causal_mask[None, None], -jnp.inf, scores)
                m = jnp.max(scores, axis=-1, keepdims=True)
                m = jnp.where(jnp.isinf(m), jnp.zeros_like(m), m)
                p = jax.nn.softmax(scores - m, axis=-1)
                oc = jnp.einsum('bhqk,bhkd->bhqd', p, v)
                return (carry, oc)
            _, outs = jax.lax.scan(body, None, (q_chunks, starts))
            return outs.transpose(1, 2, 0, 3, 4).reshape(Bq, Hq, Tq, hd)
        Bx, Tx, Dx = x.shape
        scale = 1.0 / math.sqrt(HEAD_DIM)

        def proj(W, b):
            y = x @ W.T + b
            return y.reshape(Bx, Tx, H, HEAD_DIM).transpose(0, 2, 1, 3)
        q = proj(Wq, bq)
        k = proj(Wk, bk)
        v = proj(Wv, bv)
        out = chunked_attention(q, k, v, CHUNK, scale)
        out = out.transpose(0, 2, 1, 3).reshape(Bx, Tx, Dx)
        return out @ Wo.T + bo

    def _L0_ffn_ref(x, gate_w, w1, b1, w2, b2, w3, b3, sw1, sb1, sw2, sb2, sw3, sb3):
        import jax, jax.numpy as jnp
        import numpy as np
        from jax import lax
        D_MODEL = 512
        INTER = 512
        N_EXPERTS = 8
        TOP_K = 2
        ROUTE_SCALE = 1.0
        B, S = (2, 2048)
        Bx, Sx, D = x.shape
        xt = x.reshape(-1, D)
        scores = jax.nn.softmax((xt @ gate_w.T).astype(jnp.float32), axis=-1)
        top_vals, top_idx = lax.top_k(scores, TOP_K)
        weights = (top_vals * ROUTE_SCALE).astype(x.dtype)
        combine = jnp.sum(jax.nn.one_hot(top_idx, N_EXPERTS, dtype=x.dtype) * weights[..., None], axis=1)

        def body(acc, p):
            W1, B1, W2, B2, W3, B3, c = p
            h = jax.nn.silu(xt @ W1 + B1) * (xt @ W3 + B3)
            return (acc + c[:, None] * (h @ W2 + B2), None)
        y, _ = lax.scan(body, jnp.zeros_like(xt), (w1, b1, w2, b2, w3, b3, combine.T))
        z = jax.nn.silu(xt @ sw1 + sb1) * (xt @ sw3 + sb3) @ sw2 + sb2
        return (y + z).reshape(Bx, Sx, D)
    x = x + _L0_xattn_ref(_layernorm(x, axis=-1), ctx_1024, mask_BxS2_bf0, L0_xattn_wq, L0_xattn_bq, L0_xattn_wk, L0_xattn_bk, L0_xattn_wv, L0_xattn_bv, L0_xattn_wo, L0_xattn_bo)
    x = x + _L0_attn_ref(_layernorm(x, axis=-1), L0_attn_Wq, L0_attn_bq, L0_attn_Wk, L0_attn_bk, L0_attn_Wv, L0_attn_bv, L0_attn_Wo, L0_attn_bo)
    x = x + _L0_ffn_ref(_layernorm(x, axis=-1), L0_ffn_gate_w, L0_ffn_w1, L0_ffn_b1, L0_ffn_w2, L0_ffn_b2, L0_ffn_w3, L0_ffn_b3, L0_ffn_sw1, L0_ffn_sb1, L0_ffn_sw2, L0_ffn_sb2, L0_ffn_sw3, L0_ffn_sb3)
    return x

_drawn_inputs = setup_inputs


def setup_inputs(seed=0):
    import zlib

    import numpy as np

    out = dict(_drawn_inputs(seed))
    spreads = {'L0_xattn_bq': (0.0, 0.291),
     'L0_xattn_bk': (0.0, 2.0),
     'L0_xattn_bv': (0.0, 0.1),
     'L0_xattn_bo': (0.0, 0.1),
     'L0_ffn_b1': (0.0, 0.413),
     'L0_ffn_b2': (0.0, 0.1),
     'L0_ffn_b3': (0.0, 0.41),
     'L0_ffn_sb1': (0.0, 0.1),
     'L0_ffn_sb2': (0.0, 0.1),
     'L0_ffn_sb3': (0.0, 0.1)}
    factors = {'L0_attn_bq': 29.741, 'L0_attn_bk': 64.0, 'L0_attn_bv': 4.651, 'L0_attn_bo': 6.023}
    for name, (base, spread) in spreads.items():
        noise = np.random.default_rng([zlib.crc32(name.encode()), seed]).standard_normal(out[name].shape)
        drawn = base * np.exp(spread * noise) if base else spread * noise
        out[name] = jnp.asarray(drawn.astype(out[name].dtype))
    for name, factor in factors.items():
        out[name] = (out[name] * factor).astype(out[name].dtype)
    return out
```

```python
from contextlib import ExitStack

import concourse.bass as bass
from concourse import mybir

F32 = mybir.dt.float32
F32R = mybir.dt.float32r
U8 = mybir.dt.uint8
ALU = mybir.AluOpType
ACT = mybir.ActivationFunctionType
AX = mybir.AxisListType

P = 128
BANK = 512
B, T, D = 2, 128, 512
TOK = B * T
S2 = 2048
H, HD = 16, 32
IC = D // P
HPC = P // HD
SC = float(HD) ** -0.5
EPS = 1e-5
NEG = -1.0e30

STAGES = 2 * B
HS = H // 2
OC = HS // HPC
HW = OC * P
CK = 256
NCH = S2 // CK
KT = S2 // P
PAIRS = HS // 2
STEPS = KT // 2
STAGE_STEPS = PAIRS * STEPS
LAG = 3
TB = 3
PB = 4
KROWS = 3 * HD + 1

E = 8
NE = E + 1
GATE_STEPS = 3 + 6 * B
FC = 4


def perceiver_kernel(nc, x, ctxT, mask, xwT, xbias, awT, abias, rowbias, gateT,
                     w1, w3, w2, eb, eb2, out):
    q_dram = nc.dram_tensor("q_split", [2, P, IC, TOK], F32, kind="Internal").ap()
    mask_dram = nc.dram_tensor("mask_row", [B, S2], F32, kind="Internal").ap()

    ctx = ExitStack()
    with ctx:
        def sb(name, shape, dt=F32, scope=ctx):
            return scope.enter_context(nc.sbuf_tensor(name, shape, dt))

        def sem(name):
            return ctx.enter_context(nc.semaphore(name))

        ident = sb("ident", [P, P])
        bias_x = sb("bias_x", [P, 3, IC])
        bias_a = sb("bias_a", [P, 3, IC])
        aT = sb("aT", [P, IC, TOK])
        stat = sb("stat", [P, B, 6])
        mv = sb("mv", [P, B, 2])
        std = sb("std", [P, B])
        rstd = sb("rstd", [P, B])
        epsc = sb("epsc", [P, 1])

        proj = ExitStack()
        wraw = sb("wraw", [P, 2, IC, HW], F32, proj)
        w_hi = sb("w_hi", [P, 2, IC, HW], F32R, proj)
        w_lo = sb("w_lo", [P, 2, IC, HW], F32R, proj)
        proj.close()
        wo_x = sb("wo_x", [P, IC, D])
        swq = sb("swq", [P, IC, D])
        swk = sb("swk", [P, IC, D])

        att = ExitStack()
        craw = sb("craw", [P, 2, IC, CK], F32, att)
        c_hi = sb("c_hi", [P, 2, IC, CK], F32R, att)
        c_lo = sb("c_lo", [P, 2, IC, CK], F32R, att)
        qst = sb("qst", [P, OC, HPC, T], F32R, att)
        kst = sb("kst", [P, OC, HPC, S2], F32R, att)
        v_hi = sb("v_hi", [P, KT, HW], F32R, att)
        v_lo = sb("v_lo", [P, KT, HW], F32R, att)
        pt_hi = sb("pt_hi", [P, PB, BANK], F32R, att)
        pt_lo = sb("pt_lo", [P, PB, BANK], F32R, att)
        mx = sb("mx", [P, HS, 2], F32, att)
        nmx = sb("nmx", [P, HS], F32, att)
        den = sb("den", [P, HS, 2], F32, att)
        dsum = sb("dsum", [P, HS], F32, att)
        rden = sb("rden", [P, HS], F32, att)
        rd4 = sb("rd4", [P, HS, HD], F32, att)
        oraw = sb("oraw", [P, OC, T], F32, att)
        prob = sb("prob", [P, 4, S2], F32, att)
        k_parts = [prob[:, 2 + n, :].rearrange("p (l o k) -> p l o k", l=2, o=OC) for n in range(2)]
        x_a = prob[:, 0, 0:B * D].rearrange("p (b d) -> p b d", b=B)
        xn_a = prob[:, 0, B * D:2 * B * D].rearrange("p (b d) -> p b d", b=B)
        xnT_a = prob[:, 1, 0:IC * TOK].rearrange("p (c t) -> p c t", c=IC)
        wq_a = prob[:, 2, 0:IC * D].rearrange("p (c d) -> p c d", c=IC)
        mask_u = aT[0:B, :, :].rearrange("p c t -> p (c t)").bitcast(U8)[:, 0:S2]
        mask_r = v_lo[0:B, 0:S2 // HW, :].rearrange("p k d -> p (k d)")
        mask_nan = sb("mask_nan", [B, 2], F32, att)
        q_hi = kst[:, 0, 0, 0:IC * TOK].rearrange("p (c t) -> p c t", c=IC)
        q_lo = kst[:, 0, 1, 0:IC * TOK].rearrange("p (c t) -> p c t", c=IC)
        att.close()

        late = ExitStack()
        x1 = sb("x1", [P, B, D], F32, late)
        xn = sb("xn", [P, B, D], F32, late)
        xnT = sb("xnT", [P, IC, TOK], F32, late)
        rb_x = sb("rb_x", [P, D], F32, late)
        rb_a = sb("rb_a", [P, D], F32, late)
        x3_hi = sb("x3_hi", [P, IC, TOK], F32R, late)
        x3_lo = sb("x3_lo", [P, IC, TOK], F32R, late)
        gw = sb("gw", [P, IC, E], F32, late)
        ebs = sb("ebs", [P, 2, NE, FC], F32, late)
        b2s = sb("b2s", [NE, D], F32, late)
        sc16 = sb("sc16", [P, B, 2 * E], F32, late)
        rep16 = sb("rep16", [P, B, 2 * E], F32, late)
        top8 = sb("top8", [P, B, 8], F32, late)
        gsm = sb("gsm", [P, B, 4], F32, late)
        comb = sb("comb", [P, B, NE], F32, late)
        combT = sb("combT", [NE, TOK], F32, late)
        silu = sb("silu", [P, 2, TOK], F32, late)
        gf = sb("gf", [P, 2, TOK], F32, late)
        g_hi = sb("g_hi", [P, 2, FC, TOK], F32R, late)
        g_lo = sb("g_lo", [P, 2, FC, TOK], F32R, late)
        eraw = sb("eraw", [P, 3, IC, D], F32, late)
        e_hi0 = sb("e_hi0", [P, 3, IC, D], F32R, late)
        e_lo0 = sb("e_lo0", [P, 3, IC, D], F32R, late)
        self_ = ExitStack()
        swv = sb("swv", [P, IC, D], F32, self_)
        swo = sb("swo", [P, IC, D], F32, self_)
        q_s = sb("q_s", [P, IC, TOK], F32, self_)
        k_s = sb("k_s", [P, IC, TOK], F32, self_)
        causal = sb("causal", [P, T], F32, self_)
        sc_s = sb("sc_s", [P, H, T], F32, self_)
        pt_s = sb("pt_s", [P, H, T], F32, self_)
        v_s = sb("v_s", [P, B, D], F32, self_)
        a2T = sb("a2T", [P, IC, TOK], F32, self_)
        smx = sb("smx", [P, H], F32, self_)
        srd = sb("srd", [P, H], F32, self_)
        ssum = sb("ssum", [P, H], F32, self_)
        self_.close()
        e_hi1 = sb("e_hi1", [P, 3, IC, D], F32R, late)
        e_lo1 = sb("e_lo1", [P, 3, IC, D], F32R, late)
        late.close()

        S = ctx.enter_context(nc.psum_tensor("S", [P, 4, BANK], F32))
        TP = ctx.enter_context(nc.psum_tensor("TP", [P, TB, BANK], F32))
        O = ctx.enter_context(nc.psum_tensor("O", [P, BANK], F32))

        mask_in, x_in, wq_in, bias_in = sem("mask_in"), sem("x_in"), sem("wq_in"), sem("bias_in")
        consts = sem("consts")
        ones_made = sem("ones_made")
        mask_made, mask_stored = sem("mask_made"), sem("mask_stored")
        ln_stat, ln_mv, ln_std, ln_rstd, ln_done = (sem(n) for n in ("ln_stat", "ln_mv", "ln_std", "ln_rstd", "ln_done"))
        xT_mm, xT_out = sem("xT_mm"), sem("xT_out")
        q_mm, q_hi_out, q_lo_out, q_stored = sem("q_mm"), sem("q_hi_out"), sem("q_lo_out"), sem("q_stored")
        wraw_in = [sem("wraw_in_k"), sem("wraw_in_v")]
        craw_in = [sem("craw_in_0"), sem("craw_in_1")]
        w_hi_made, w_made = sem("w_hi_made"), sem("w_made")
        c_hi_made, c_made = sem("c_hi_made"), sem("c_made")
        k_mm, k_hi_out, k_out = sem("k_mm"), sem("k_hi_out"), sem("k_out")
        k_stacked = [[sem(f"k_stacked_{g}_{n}") for n in range(2)] for g in range(HPC)]
        v_mm, v_hi_out, v_out = sem("v_mm"), sem("v_hi_out"), sem("v_out")
        q_stacked = sem("q_stacked")
        s_mm, mx_half, nmx_made, exp_done = sem("s_mm"), sem("mx_half"), sem("nmx_made"), sem("exp_done")
        t_mm, pt_hi_out, pt_out, pv_mm, o_out = sem("t_mm"), sem("pt_hi_out"), sem("pt_out"), sem("pv_mm"), sem("o_out")
        dsum_made, rden_made, rd4_made, rb_mm = sem("dsum_made"), sem("rden_made"), sem("rd4_made"), sem("rb_mm")
        o_normed, a_done = sem("o_normed"), sem("a_done")
        late_w = [sem(f"late_w{i}") for i in range(5)]
        x1_in, row_in, ffn_small_in = sem("x1_in"), sem("row_in"), sem("ffn_small_in")
        bo_added, oproj_mm, x1_done = sem("bo_added"), sem("oproj_mm"), sem("x1_done")
        sp_mm, sp_out = sem("sp_mm"), sem("sp_out")
        ss_mm, ss_masked, ss_max, ss_sub, ss_exp = (sem(n) for n in ("ss_mm", "ss_masked", "ss_max", "ss_sub", "ss_exp"))
        ss_sum, ss_rd, ss_normed, sT_mm, sT_out = (sem(n) for n in ("ss_sum", "ss_rd", "ss_normed", "sT_mm", "sT_out"))
        so_mm, so_out, bo2_added, oproj2_mm, x2_done = (sem(n) for n in ("so_mm", "so_out", "bo2_added", "oproj2_mm", "x2_done"))
        x3_hi_made, x3_made = sem("x3_hi_made"), sem("x3_made")
        gate_mm, gate_step, gate_exp, combT_mm, combT_out, b2_mm, acc_step = (
            sem(n) for n in ("gate_mm", "gate_step", "gate_exp", "combT_mm", "combT_out", "b2_mm", "acc_step"))
        eraw_in = [sem(f"eraw_in_{n}") for n in ("w1", "w3", "w2")]
        e_hi_made, e_made = sem("e_hi_made"), sem("e_made")
        h_mm, silu_made, g_made, g_hi_made, g_split, y_mm = (
            sem(n) for n in ("h_mm", "silu_made", "g_made", "g_hi_made", "g_split", "y_mm"))
        out_stored = sem("out_stored")

        KST = 3 * 16
        QST = (3 * HPC + 1) * 16
        PROJ = [x for c in range(NCH - 2) for x in (("K", c), ("V", c))] + [
            ("K", NCH - 2), ("K", NCH - 1), ("V", NCH - 2), ("S", 0), ("V", NCH - 1), ("S", 1)]

        def f32(ap):
            return ap.bitcast(F32)

        def all_stages(eng, first, stage):
            first()
            stage(0, False)
            with eng.Fori(1, STAGES - 1) as s:
                stage(s, False)
            stage(STAGES - 1, True)

        def all_experts(eng, expert):
            expert(0, 0, True, False)
            expert(1, 1, False, False)
            with eng.Fori(1, NE // 2) as k:
                expert(2 * k, 0, False, False)
                expert(2 * k + 1, 1, False, False)
            expert(NE - 1, 0, False, True)

        def e_hi(slot):
            return (e_hi0, e_hi1)[slot]

        def e_lo(slot):
            return (e_lo0, e_lo1)[slot]

        block = ctx.enter_context(nc.Block())

        @block.sync
        def _(sp):
            def first():
                sp.dma_start(x_a, x.rearrange("b t d -> t b d")).then_inc(x_in, 16)
                sp.dma_start(wq_a, xwT[0]).then_inc(wq_in, 16)
                sp.dma_start(bias_x[:, :, :], xbias).then_inc(bias_in, 16)
                sp.dma_start(bias_a[:, :, :], abias).then_inc(bias_in, 16)
                sp.dma_start(mask_u, mask).then_inc(mask_in, 16)
                sp.wait_ge(mask_made, 5)
                sp.dma_start(mask_dram, f32(mask_r)).then_inc(mask_stored, 16)
                sp.wait_ge(q_lo_out, 2)
                sp.dma_start(q_dram[0], f32(q_hi)).then_inc(q_stored, 16)
                sp.dma_start(q_dram[1], f32(q_lo)).then_inc(q_stored, 16)
                sp.wait_ge(mask_stored, 16)
                sp.wait_ge(q_stored, 32)

            def stage(s, last):
                b, half = s // 2, s % 2
                for c in range(NCH):
                    if c == 0:
                        sp.wait_ge(s_mm, 2 * HS * s)
                        for g in range(HPC):
                            rows = slice(g * HD, (g + 1) * HD)
                            for at, part in ((0, 0), (HD, 0), (2 * HD, 1)):
                                sp.dma_start(f32(qst[at:at + HD, :, g, :]),
                                             q_dram[part][rows, bass.ds(half * OC, OC), bass.ds(b * T, T)]
                                             ).then_inc(q_stacked, 16)
                        sp.dma_start(f32(kst[3 * HD:KROWS, :, :, :]).rearrange("p o g k -> p (o g) k"),
                                     mask_dram[bass.ds(b, 1), :].unsqueeze(1).to_broadcast([1, HS, S2])
                                     ).then_inc(q_stacked, 16)
                    if c % 2:
                        sp.wait_ge(k_out, s * NCH + c + 1)
                        for g in range(HPC):
                            rows = slice(g * HD, (g + 1) * HD)
                            for at, part in ((0, 0), (HD, 1), (2 * HD, 0)):
                                sp.dma_start(f32(kst[at:at + HD, :, g, (c - 1) * CK:(c + 1) * CK]),
                                             k_parts[c // 2 % 2][rows, part]).then_inc(k_stacked[g][c // 2 % 2], 16)

            all_stages(sp, first, stage)

            sp.wait_ge(v_mm, STAGES * NCH)
            sp.dma_start(wo_x[:, :, :], xwT[3]).then_inc(late_w[0], 16)
            sp.dma_start(swq[:, :, :], awT[0]).then_inc(late_w[1], 16)
            sp.dma_start(swk[:, :, :], awT[1]).then_inc(late_w[2], 16)
            sp.wait_ge(a_done, STAGES * OC)
            sp.dma_start(x1[:, :, :], x.rearrange("b t d -> t b d")).then_inc(x1_in, 16)
            sp.dma_start(rb_x[:, :], rowbias[0].partition_broadcast(P)).then_inc(row_in, 16)
            sp.dma_start(rb_a[:, :], rowbias[1].partition_broadcast(P)).then_inc(row_in, 16)
            sp.dma_start(swv[:, :, :], awT[2]).then_inc(late_w[3], 16)
            sp.dma_start(swo[:, :, :], awT[3]).then_inc(late_w[4], 16)
            sp.dma_start(gw[:, :, :], gateT).then_inc(ffn_small_in, 16)
            sp.dma_start(ebs[:, :, :, :], eb).then_inc(ffn_small_in, 16)
            sp.dma_start(b2s[:, :], eb2).then_inc(ffn_small_in, 16)

            def expert(e, slot, first_one, last_one):
                for k, w in enumerate((w1, w3, w2)):
                    if not first_one:
                        sp.wait_ge(e_made, 3 * e + k - 2)
                    sp.dma_start(eraw[:, k], w[e] if isinstance(e, int) else w[bass.ds(e, 1)].rearrange(
                        "e p c d -> (e p) c d")).then_inc(eraw_in[k], 16)

            all_experts(sp, expert)
            sp.wait_ge(acc_step, B * (NE + 1))
            sp.dma_start(out.rearrange("b t d -> t b d"), x1[:, :, :]).then_inc(out_stored, 16)
            sp.wait_ge(out_stored, 16)

        @block.gpsimd
        def _(pool):
            nc.gpsimd.memset(ident[:, :], 0.0).then_inc(consts, 1)
            nc.gpsimd.memset(epsc[:, :], EPS).then_inc(consts, 1)
            pool.wait_ge(consts, 2)
            nc.gpsimd.affine_select(out=ident[:, :], in_=ident[:, :], compare_op=ALU.not_equal, fill=1.0,
                                    base=0, pattern=[[-1, P]], channel_multiplier=1).then_inc(consts, 1)
            pool.wait_ge(a_done, STAGES * OC)
            nc.gpsimd.memset(causal[:, :], 0.0).then_inc(consts, 1)
            pool.wait_ge(consts, 4)
            nc.gpsimd.affine_select(out=causal[:, :], in_=causal[:, :], compare_op=ALU.is_ge, fill=NEG,
                                    base=0, pattern=[[-1, T]], channel_multiplier=1).then_inc(consts, 1)

        @block.tensor
        def _(pe):
            def products(out_ap, a, b):
                for ic in range(IC):
                    (ah, al), (bh, bl) = a(ic), b(ic)
                    for n, (l, r) in enumerate(((ah, bh), (ah, bl), (al, bh))):
                        mm = nc.tensor.matmul(out_ap, l, r, start=(ic == 0 and n == 0),
                                              stop=(ic == IC - 1 and n == 2))
                return mm

            def plain(out_ap, a, b):
                for ic in range(IC):
                    mm = nc.tensor.matmul(out_ap, a(ic), b(ic), start=(ic == 0), stop=(ic == IC - 1))
                return mm

            def transpose_x(n, src):
                for b in range(B):
                    pe.wait_ge(ln_done, B * n + b + 1)
                    for ic in range(IC):
                        mm = nc.tensor.transpose(TP[:, b, ic * P:(ic + 1) * P], src[:, b, ic * P:(ic + 1) * P],
                                                 ident[:, :])
                    mm.then_inc(xT_mm, 1)

            def first():
                pe.wait_ge(consts, 3)
                pe.wait_ge(ones_made, 1)
                transpose_x(0, xn_a)
                pe.wait_ge(wq_in, 16)
                pe.wait_ge(xT_out, B)
                for oc in range(IC):
                    mm = plain(S[:, oc // 2, (oc % 2) * TOK:(oc % 2 + 1) * TOK],
                               lambda ic: wq_a[:, ic, oc * P:(oc + 1) * P], lambda ic: xnT_a[:, ic, :])
                    if oc % 2:
                        mm.then_inc(q_mm, 1)

            def project_k(s, c):
                if c == 0:
                    pe.wait_ge(w_made, 2 * s + 2)
                pe.wait_ge(c_made, s * NCH + c + 1)
                if c >= 2:
                    pe.wait_ge(k_out, s * NCH + c - 1)
                for o in range(OC):
                    cols = slice(o * P, (o + 1) * P)
                    mm = products(TP[:, c % 2, o * CK:(o + 1) * CK],
                                  lambda ic: (w_hi[:, 0, ic, cols], w_lo[:, 0, ic, cols]),
                                  lambda ic: (c_hi[:, c % 2, ic, :], c_lo[:, c % 2, ic, :]))
                mm.then_inc(k_mm, 1)

            def project_v(s, c):
                bank = TP[:, 2, :] if c % 2 == 0 else O[:, :]
                if c >= 2:
                    pe.wait_ge(v_out, s * NCH + c - 1)
                if c == 1:
                    pe.wait_ge(o_out, s * PAIRS)
                for k in range(CK // P):
                    keys = slice(k * P, (k + 1) * P)
                    mm = products(bank[:, k * HW:(k + 1) * HW],
                                  lambda ic: (c_hi[:, c % 2, ic, keys], c_lo[:, c % 2, ic, keys]),
                                  lambda ic: (w_hi[:, 1, ic, :], w_lo[:, 1, ic, :]))
                mm.then_inc(v_mm, 1)

            def scores(s, h):
                if h < HPC:
                    for n in range(2):
                        pe.wait_ge(k_stacked[h][n], KST * (NCH // 4) * (s + 1))
                if h == 0:
                    pe.wait_ge(q_stacked, QST * (s + 1))
                    pe.wait_ge(o_normed, s)
                for n in range(4):
                    if n == 0 and h == 0:
                        pe.wait_ge(exp_done, 2 * HS * s)
                    elif n % 2 == 0 and h > 0:
                        pe.wait_ge(exp_done, 2 * (HS * s + h) - 1 + n // 2)
                    mm = nc.tensor.matmul(S[:, n, :], qst[0:KROWS, h // HPC, h % HPC, :],
                                          kst[0:KROWS, h // HPC, h % HPC, n * BANK:(n + 1) * BANK],
                                          start=True, stop=True)
                    if n % 2:
                        mm.then_inc(s_mm, 1)

            def transposes(s, g):
                p, j = g // STEPS, g % STEPS
                if j == 0:
                    pe.wait_ge(exp_done, 2 * (HS * s + 2 * p + 2))
                if g >= TB:
                    pe.wait_ge(pt_out, s * STAGE_STEPS + g - TB + 1)
                elif g == 0:
                    pe.wait_ge(k_out, (s + 1) * NCH)
                elif g == 2:
                    pe.wait_ge(v_out, s * NCH + NCH - 1)
                for k in range(2):
                    for hl in range(2):
                        kt = 2 * j + k
                        mm = nc.tensor.transpose(TP[:, g % TB, (2 * k + hl) * P:(2 * k + hl + 1) * P],
                                                 prob[:, (2 * p + hl) % 4, kt * P:(kt + 1) * P], ident[:, :])
                mm.then_inc(t_mm, 1)

            def times_v(s, g):
                p, j = g // STEPS, g % STEPS
                pe.wait_ge(pt_out, s * STAGE_STEPS + g + 1)
                if g == 0:
                    pe.wait_ge(v_out, (s + 1) * NCH)
                elif j == 0:
                    pe.wait_ge(o_out, s * PAIRS + p)
                cols = slice((p // 2) * P, (p // 2 + 1) * P)
                for k in range(2):
                    kt, pc = 2 * j + k, slice(k * 2 * P, (k + 1) * 2 * P)
                    for n, (l, r) in enumerate(((v_hi, pt_hi), (v_hi, pt_lo), (v_lo, pt_hi))):
                        mm = nc.tensor.matmul(O[:, 0:2 * P], l[:, kt, cols], r[:, g % PB, pc],
                                              start=(kt == 0 and n == 0), stop=(kt == KT - 1 and n == 2))
                mm.then_inc(pv_mm, 1)

            def stage(s, last):
                for what, n in PROJ:
                    {"K": project_k, "V": project_v, "S": scores}[what](s, n)
                for g in range(STAGE_STEPS + LAG):
                    if g < STAGE_STEPS:
                        p, j = g // STEPS, g % STEPS
                        if j in (1, 5) and p < PAIRS - 1:
                            scores(s, 2 * p + 2 + (j == 5))
                        transposes(s, g)
                        if g == STAGE_STEPS - 3:
                            pe.wait_ge(rd4_made, s + 1)
                            for o in range(OC):
                                mm = nc.tensor.matmul(S[:, 0, o * P:(o + 1) * P],
                                                      rd4[:, o * HPC:(o + 1) * HPC, :].rearrange("p h d -> p (h d)"),
                                                      ident[:, :], start=True, stop=True)
                            mm.then_inc(rb_mm, 1)
                    if g >= LAG:
                        times_v(s, g - LAG)

            all_stages(pe, first, stage)

            pe.wait_ge(a_done, STAGES * OC)
            pe.wait_ge(late_w[0], 16)
            for b in range(B):
                plain(S[:, b, :], lambda ic: aT[:, ic, b * T:(b + 1) * T], lambda ic: wo_x[:, ic, :]).then_inc(oproj_mm, 1)
            transpose_x(1, xn)
            pe.wait_ge(xT_out, 2 * B)
            pe.wait_ge(x1_done, B)
            for n, w in enumerate((swq, swk)):
                pe.wait_ge(late_w[1 + n], 16)
                for oc in range(IC):
                    mm = plain(S[:, 2 * n + oc // 2, (oc % 2) * TOK:(oc % 2 + 1) * TOK],
                               lambda ic: w[:, ic, oc * P:(oc + 1) * P], lambda ic: xnT[:, ic, :])
                    if oc % 2:
                        mm.then_inc(sp_mm, 1)
            pe.wait_ge(late_w[3], 16)
            for b in range(B):
                plain(TP[:, b, :], lambda ic: xnT[:, ic, b * T:(b + 1) * T], lambda ic: swv[:, ic, :]).then_inc(sp_mm, 1)
            for b in range(B):
                if b == 0:
                    pe.wait_ge(sp_out, 6)
                else:
                    pe.wait_ge(ss_masked, b)
                for h in range(H):
                    g, oc = h % HPC, h // HPC
                    mm = nc.tensor.matmul(S[:, g, oc * T:(oc + 1) * T],
                                          q_s[g * HD:(g + 1) * HD, oc, b * T:(b + 1) * T],
                                          k_s[g * HD:(g + 1) * HD, oc, b * T:(b + 1) * T], start=True, stop=True)
                mm.then_inc(ss_mm, 1)
                pe.wait_ge(ss_normed, b + 1)
                for n in range(4):
                    if n == 3 or b > 0:
                        pe.wait_ge(sT_out, 4 * b + n)
                    for i in range(4):
                        mm = nc.tensor.transpose(TP[:, n % 2, i * T:(i + 1) * T], sc_s[:, 4 * n + i, :], ident[:, :])
                    mm.then_inc(sT_mm, 1)
                    if n == 1:
                        pe.wait_ge(sT_out, 4 * b + 1)
                    if n == 2:
                        pe.wait_ge(sT_out, 4 * b + 2)
                pe.wait_ge(sT_out, 4 * b + 4)
                if b > 0:
                    pe.wait_ge(so_out, b)
                for h in range(H):
                    g, oc = h % HPC, h // HPC
                    mm = nc.tensor.matmul(TP[g * HD:(g + 1) * HD, 2, oc * T:(oc + 1) * T],
                                          v_s[:, b, h * HD:(h + 1) * HD], pt_s[:, g * IC + oc, :],
                                          start=True, stop=True)
                mm.then_inc(so_mm, 1)
            pe.wait_ge(so_out, B)
            pe.wait_ge(ss_masked, B)
            pe.wait_ge(late_w[4], 16)
            for b in range(B):
                plain(S[:, b, :], lambda ic: a2T[:, ic, b * T:(b + 1) * T], lambda ic: swo[:, ic, :]).then_inc(oproj2_mm, 1)
            transpose_x(2, xn)
            pe.wait_ge(ffn_small_in, 48)
            pe.wait_ge(xT_out, 3 * B)
            for b in range(B):
                mm = plain(TP[:, 2, b * E:(b + 1) * E], lambda ic: xnT[:, ic, b * T:(b + 1) * T], lambda ic: gw[:, ic, :])
            mm.then_inc(gate_mm, 1)

            def second_biases():
                pe.wait_ge(gate_step, GATE_STEPS)
                for b in range(B):
                    mm = nc.tensor.transpose(TP[0:NE, 2, b * T:(b + 1) * T], comb[:, b, :], ident[:, :])
                mm.then_inc(combT_mm, 1)
                pe.wait_ge(combT_out, 1)
                for b in range(B):
                    mm = nc.tensor.matmul(S[:, B + b, :], combT[:, b * T:(b + 1) * T], b2s[:, :], start=True, stop=True)
                mm.then_inc(b2_mm, 1)

            def up(e, slot, f):
                if f == 0:
                    pe.wait_ge(e_made, 3 * e + 2)
                if f >= 2 or not isinstance(e, int) or e > 0:
                    pe.wait_ge(g_made, FC * e + f - 1)
                else:
                    pe.wait_ge(x3_made, B)
                for n in range(2):
                    cols = slice(f * P, (f + 1) * P)
                    mm = products(TP[:, f % 2, n * TOK:(n + 1) * TOK],
                                  lambda ic: (e_hi(slot)[:, n, ic, cols], e_lo(slot)[:, n, ic, cols]),
                                  lambda ic: (x3_hi[:, ic, :], x3_lo[:, ic, :]))
                mm.then_inc(h_mm, 1)

            def down(e, slot):
                pe.wait_ge(g_split, FC * e + FC)
                pe.wait_ge(e_made, 3 * e + 3)
                pe.wait_ge(acc_step, B * e)
                for b in range(B):
                    mm = products(S[:, 2 * slot + b, :],
                                  lambda ic: (g_hi[:, slot, ic, b * T:(b + 1) * T], g_lo[:, slot, ic, b * T:(b + 1) * T]),
                                  lambda ic: (e_hi(slot)[:, 2, ic, :], e_lo(slot)[:, 2, ic, :]))
                    mm.then_inc(y_mm, 1)

            def expert(e, slot, first_one, last_one):
                up(e, slot, 0)
                if not first_one:
                    down(e - 1, 1 - slot)
                for f in range(1, FC):
                    up(e, slot, f)
                if first_one:
                    second_biases()
                if last_one:
                    down(e, slot)

            all_experts(pe, expert)

        @block.scalar
        def _(act):
            def load_w(s):
                act.wait_ge(w_made, 2 * s)
                for n in range(2):
                    act.dma_start(wraw[:, n], xwT[1 + n][:, :, bass.ds((s % 2) * HW, HW)]).then_inc(wraw_in[n], 16)

            def load_c(s, c):
                act.dma_start(craw[:, c % 2], ctxT[s // 2, c]).then_inc(craw_in[c % 2], 16)

            def ln_sqrt(n):
                act.wait_ge(ln_mv, B * (n + 1))
                nc.scalar.activation(std[:, :], mv[:, :, 1], ACT.Sqrt, bias=epsc[:, 0:1]).then_inc(ln_std, 1)

            def split_w(s):
                for n in range(2):
                    act.wait_ge(wraw_in[n], 16 * s + 16)
                    nc.scalar.copy(w_hi[:, n], wraw[:, n]).then_inc(w_hi_made, 1)

            def split_c(s, c):
                act.wait_ge(craw_in[c % 2], 16 * (s * (NCH // 2) + c // 2 + 1))
                nc.scalar.copy(c_hi[:, c % 2], craw[:, c % 2]).then_inc(c_hi_made, 1)

            def first():
                load_w(0)
                load_c(0, 0)
                load_c(0, 1)
                act.wait_ge(consts, 2)
                ln_sqrt(0)
                act.wait_ge(bias_in, 32)
                for n in range(2):
                    act.wait_ge(q_mm, n + 1)
                    for o in range(2):
                        oc = 2 * n + o
                        i = nc.scalar.activation(q_hi[:, oc, :], S[:, n, o * TOK:(o + 1) * TOK], ACT.Identity,
                                                 bias=bias_x[:, 0, oc:oc + 1])
                    i.then_inc(q_hi_out, 1)
                split_w(0)
                split_c(0, 0)
                split_c(0, 1)

            def exps(s, h):
                act.wait_ge(nmx_made, s * HS + h + 1)
                if h == 0:
                    act.wait_ge(t_mm, s * STAGE_STEPS)
                elif h >= 4:
                    act.wait_ge(t_mm, s * STAGE_STEPS + (h // 2 - 1) * STEPS)
                for n in range(2):
                    nc.scalar.activation(prob[:, h % 4, n * 2 * BANK:(n + 1) * 2 * BANK],
                                         S[:, 2 * n:2 * n + 2, :].rearrange("p n k -> p (n k)"), ACT.Exp,
                                         bias=nmx[:, h:h + 1], scale=SC,
                                         accum_out=den[:, h, n:n + 1]).then_inc(exp_done, 1)

            def stage(s, last):
                for what, n in PROJ:
                    if what == "K":
                        if n + 2 < NCH or not last:
                            act.wait_ge(c_made, s * NCH + n + 1)
                            load_c(s + (n + 2) // NCH, (n + 2) % NCH)
                        if n == 1 and not last:
                            load_w(s + 1)
                    elif what == "V":
                        act.wait_ge(v_mm, s * NCH + n + 1)
                        src = TP[:, 2, :] if n % 2 == 0 else O[:, :]
                        nc.scalar.copy(v_hi[:, 2 * n:2 * n + 2, :].rearrange("p k d -> p (k d)"), src).then_inc(v_hi_out, 1)
                        if n + 2 < NCH:
                            split_c(s, n + 2)
                    elif what == "S":
                        exps(s, n)
                for g in range(STAGE_STEPS):
                    p, j = g // STEPS, g % STEPS
                    act.wait_ge(t_mm, s * STAGE_STEPS + g + 1)
                    if g >= PB:
                        act.wait_ge(pv_mm, s * STAGE_STEPS + g - PB + 1)
                    nc.scalar.copy(pt_hi[:, g % PB, :], TP[:, g % TB, :]).then_inc(pt_hi_out, 1)
                    if j in (3, 7) and p < PAIRS - 1:
                        exps(s, 2 * p + 2 + (j == 7))
                    if g == STAGE_STEPS - 6 and not last:
                        split_w(s + 1)
                        split_c(s + 1, 0)
                    if g == STAGE_STEPS - 4 and not last:
                        split_c(s + 1, 1)

            all_stages(act, first, stage)

            ln_sqrt(1)
            for n in range(2):
                act.wait_ge(sp_mm, n + 1)
                for o in range(2):
                    oc = 2 * n + o
                    i = nc.scalar.activation(q_s[:, oc, :], S[:, n, o * TOK:(o + 1) * TOK], ACT.Identity,
                                             bias=bias_a[:, 0, oc:oc + 1])
                i.then_inc(sp_out, 1)
            for b in range(B):
                act.wait_ge(sp_mm, 5 + b)
                nc.scalar.copy(v_s[:, b, :], TP[:, b, :]).then_inc(sp_out, 1)
            for b in range(B):
                act.wait_ge(ss_sub, b + 1)
                nc.scalar.activation(sc_s[:, :, :], sc_s[:, :, :], ACT.Exp, scale=SC).then_inc(ss_exp, 1)
                for n in range(0, 4, 2):
                    act.wait_ge(sT_mm, 4 * b + n + 1)
                    nc.scalar.copy(pt_s[:, 4 * n:4 * n + 4, :].rearrange("p h t -> p (h t)"), TP[:, 0, :]).then_inc(sT_out, 1)
                    act.wait_ge(sT_out, 4 * b + n + 1)
            ln_sqrt(2)

            def split_e(e, slot, k):
                act.wait_ge(eraw_in[k], 16 * e + 16)
                if not isinstance(e, int) or e >= 2:
                    if k < 2:
                        act.wait_ge(h_mm, FC * (e - 1))
                    else:
                        act.wait_ge(y_mm, B * (e - 1))
                nc.scalar.copy(e_hi(slot)[:, k], eraw[:, k]).then_inc(e_hi_made, 1)

            for b in range(B):
                act.wait_ge(xT_mm, 2 * B + b + 1)
                nc.scalar.copy(x3_hi[:, :, b * T:(b + 1) * T], TP[:, b, :].rearrange("p (c t) -> p c t", c=IC)).then_inc(x3_hi_made, 1)
            for k in range(3):
                split_e(0, 0, k)
            act.wait_ge(gate_step, 1)
            for b in range(B):
                nc.scalar.activation(sc16[:, b, 0:E], TP[:, 2, b * E:(b + 1) * E], ACT.Exp,
                                     bias=gsm[:, b, 0:1], accum_out=gsm[:, b, 1:2]).then_inc(gate_exp, 1)

            def expert(e, slot, first_one, last_one):
                for f in range(FC):
                    act.wait_ge(h_mm, FC * e + f + 1)
                    act.wait_ge(ffn_small_in, 48)
                    nc.scalar.activation(silu[:, f % 2, :], TP[:, f % 2, 0:TOK], ACT.Silu,
                                         bias=ebs[:, 0, bass.ds(e, 1), f]).then_inc(silu_made, 1)
                    act.wait_ge(g_made, FC * e + f + 1)
                    if f == 0 and (not isinstance(e, int) or e >= 2):
                        act.wait_ge(y_mm, B * (e - 1))
                    nc.scalar.copy(g_hi[:, slot, f, :], gf[:, f % 2, :]).then_inc(g_hi_made, 1)
                    if f < 3 and not last_one:
                        split_e(e + 1, 1 - slot, f)

            all_experts(act, expert)

        @block.vector
        def _(dve):
            def layer_norm(n, src, dst):
                for b in range(B):
                    nc.vector.bn_stats(stat[:, b, :], src[:, b, :]).then_inc(ln_stat, 1)
                for b in range(B):
                    dve.wait_ge(ln_stat, B * n + b + 1)
                    nc.vector.bn_aggr(mv[:, b, :], stat[:, b, :]).then_inc(ln_mv, 1)
                dve.wait_ge(ln_std, n + 1)
                nc.vector.reciprocal(rstd[:, :], std[:, :]).then_inc(ln_rstd, 1)
                dve.wait_ge(ln_rstd, n + 1)
                for b in range(B):
                    nc.vector.tensor_scalar(dst[:, b, :], src[:, b, :], mv[:, b, 0:1], rstd[:, b:b + 1],
                                            ALU.subtract, ALU.mult).then_inc(ln_done, 1)

            def transposed_out(n, dst):
                for b in range(B):
                    dve.wait_ge(xT_mm, B * n + b + 1)
                    if n == 2:
                        dve.wait_ge(x3_hi_made, b + 1)
                    nc.vector.tensor_copy(dst[:, :, b * T:(b + 1) * T],
                                          TP[:, b, :].rearrange("p (c t) -> p c t", c=IC)).then_inc(xT_out, 1)

            def split_w(s):
                for n in range(2):
                    dve.wait_ge(w_hi_made, 2 * s + n + 1)
                    nc.vector.tensor_tensor(w_lo[:, n], wraw[:, n], f32(w_hi[:, n]), ALU.subtract).then_inc(w_made, 1)

            def split_c(s, c):
                dve.wait_ge(c_hi_made, s * NCH + c + 1)
                nc.vector.tensor_tensor(c_lo[:, c % 2], craw[:, c % 2], f32(c_hi[:, c % 2]), ALU.subtract).then_inc(c_made, 1)

            def first():
                nc.vector.memset(f32(qst[3 * HD:KROWS, :, :, :]), 1.0).then_inc(ones_made, 1)
                dve.wait_ge(x_in, 16)
                layer_norm(0, x_a, xn_a)
                transposed_out(0, xnT_a)
                dve.wait_ge(mask_in, 16)
                nc.vector.tensor_reduce(mask_nan[:, 0:1], mask_u, AX.X, ALU.min).then_inc(mask_made, 1)
                dve.wait_ge(mask_made, 1)
                nc.vector.tensor_scalar(mask_nan[:, 0:1], mask_nan[:, 0:1], -3.0e38, 10.0, ALU.mult, ALU.mult).then_inc(mask_made, 1)
                dve.wait_ge(mask_made, 2)
                nc.vector.tensor_tensor(mask_nan[:, 1:2], mask_nan[:, 0:1], mask_nan[:, 0:1], ALU.subtract).then_inc(mask_made, 1)
                dve.wait_ge(mask_made, 3)
                nc.vector.tensor_scalar(mask_r, mask_u, NEG, mask_nan[:, 1:2], ALU.mult, ALU.add).then_inc(mask_made, 2)
                dve.wait_ge(bias_in, 32)
                for n in range(2):
                    dve.wait_ge(q_hi_out, n + 1)
                    for o in range(2):
                        oc = 2 * n + o
                        i = nc.vector.scalar_tensor_tensor(q_lo[:, oc, :], S[:, n, o * TOK:(o + 1) * TOK],
                                                           bias_x[:, 0, oc:oc + 1], f32(q_hi[:, oc, :]),
                                                           ALU.add, ALU.subtract)
                    i.then_inc(q_lo_out, 1)
                split_w(0)
                split_c(0, 0)
                split_c(0, 1)
                dve.wait_ge(mask_stored, 16)

            def maxima(s, h):
                if h == 0:
                    dve.wait_ge(exp_done, 2 * HS * s)
                for n in range(2):
                    dve.wait_ge(s_mm, 2 * (s * HS + h) + n + 1)
                    nc.vector.tensor_reduce(mx[:, h, n:n + 1], S[:, 2 * n:2 * n + 2, :].rearrange("p n k -> p (n k)"),
                                            AX.X, ALU.max).then_inc(mx_half, 1)
                dve.wait_ge(mx_half, 2 * (s * HS + h) + 2)
                nc.vector.tensor_scalar(nmx[:, h:h + 1], mx[:, h, 0:1], mx[:, h, 1:2], -SC,
                                        ALU.max, ALU.mult).then_inc(nmx_made, 1)

            def outputs_out(s, p):
                dve.wait_ge(pv_mm, s * STAGE_STEPS + (p + 1) * STEPS)
                if p == 0:
                    dve.wait_ge(o_normed, s)
                for hl in range(2):
                    g = (2 * p + hl) % HPC
                    i = nc.vector.tensor_copy(oraw[g * HD:(g + 1) * HD, p // 2, :],
                                              O[g * HD:(g + 1) * HD, hl * T:(hl + 1) * T])
                i.then_inc(o_out, 1)

            def spread_sums(s):
                dve.wait_ge(exp_done, 2 * HS * (s + 1))
                nc.vector.tensor_tensor(dsum[:, :], den[:, :, 0], den[:, :, 1], ALU.add).then_inc(dsum_made, 1)
                dve.wait_ge(dsum_made, s + 1)
                nc.vector.reciprocal(rden[:, :], dsum[:, :]).then_inc(rden_made, 1)
                dve.wait_ge(rden_made, s + 1)
                nc.vector.tensor_copy(rd4[:, :, :], rden[:, :].unsqueeze(2).to_broadcast([P, HS, HD])).then_inc(rd4_made, 1)

            def stage(s, last):
                for what, n in PROJ:
                    if what == "K":
                        dve.wait_ge(k_mm, s * NCH + n + 1)
                        part = [k_parts[n // 2 % 2][:, l, :, (n % 2) * CK:(n % 2 + 1) * CK] for l in range(2)]
                        if n % 2 == 0 and n >= 4:
                            for g in range(HPC):
                                dve.wait_ge(k_stacked[g][n // 2 % 2], KST * (s * (NCH // 4) + n // 4))
                        elif n == 0:
                            dve.wait_ge(t_mm, s * STAGE_STEPS)
                            dve.wait_ge(q_stored, 32)
                        for o in range(OC):
                            i = nc.vector.tensor_scalar(part[0][:, o].bitcast(F32R), TP[:, n % 2, o * CK:(o + 1) * CK],
                                                        bias_x[:, 1, bass.ds((s % 2) * OC + o, 1)], None, ALU.add)
                        i.then_inc(k_hi_out, 1)
                        dve.wait_ge(k_hi_out, s * NCH + n + 1)
                        for o in range(OC):
                            i = nc.vector.scalar_tensor_tensor(part[1][:, o].bitcast(F32R), TP[:, n % 2, o * CK:(o + 1) * CK],
                                                               bias_x[:, 1, bass.ds((s % 2) * OC + o, 1)],
                                                               part[0][:, o], ALU.add, ALU.subtract)
                        i.then_inc(k_out, 1)
                    elif what == "V":
                        dve.wait_ge(v_hi_out, s * NCH + n + 1)
                        src = TP[:, 2, :] if n % 2 == 0 else O[:, :]
                        nc.vector.tensor_tensor(v_lo[:, 2 * n:2 * n + 2, :].rearrange("p k d -> p (k d)"), src,
                                                f32(v_hi[:, 2 * n:2 * n + 2, :]).rearrange("p k d -> p (k d)"),
                                                ALU.subtract).then_inc(v_out, 1)
                        if n + 2 < NCH:
                            split_c(s, n + 2)
                    else:
                        maxima(s, n)
                for g in range(STAGE_STEPS):
                    p, j = g // STEPS, g % STEPS
                    dve.wait_ge(pt_hi_out, s * STAGE_STEPS + g + 1)
                    nc.vector.tensor_tensor(pt_lo[:, g % PB, :], TP[:, g % TB, :], f32(pt_hi[:, g % PB, :]),
                                            ALU.subtract).then_inc(pt_out, 1)
                    if j == LAG - 1 and p > 0:
                        outputs_out(s, p - 1)
                    if j in (1, 5) and p < PAIRS - 1:
                        maxima(s, 2 * p + 2 + (j == 5))
                    if p == PAIRS - 1 and j == 1:
                        spread_sums(s)
                    if g == STAGE_STEPS - 6 and not last:
                        split_w(s + 1)
                        split_c(s + 1, 0)
                    if g == STAGE_STEPS - 4 and not last:
                        split_c(s + 1, 1)
                outputs_out(s, PAIRS - 1)
                dve.wait_ge(rb_mm, s + 1)
                dve.wait_ge(o_out, (s + 1) * PAIRS)
                nc.vector.tensor_tensor(oraw[:, :, :].rearrange("p o t -> p (o t)"), S[:, 0, 0:OC * P],
                                        oraw[:, :, :].rearrange("p o t -> p (o t)"), ALU.mult).then_inc(o_normed, 1)
                dve.wait_ge(o_normed, s + 1)
                for o in range(OC):
                    nc.vector.tensor_scalar(aT[:, bass.ds((s % 2) * OC + o, 1), bass.ds((s // 2) * T, T)], oraw[:, o:o + 1, :],
                                            bias_x[:, 2, bass.ds((s % 2) * OC + o, 1)], None, ALU.add).then_inc(a_done, 1)

            all_stages(dve, first, stage)

            dve.wait_ge(x1_in, 16)
            dve.wait_ge(row_in, 32)
            nc.vector.tensor_tensor(x1[:, :, :], x1[:, :, :], rb_x[:, :].unsqueeze(1).to_broadcast([P, B, D]), ALU.add).then_inc(bo_added, 1)
            dve.wait_ge(bo_added, 1)
            for b in range(B):
                dve.wait_ge(oproj_mm, b + 1)
                nc.vector.tensor_tensor(x1[:, b, :], S[:, b, :], x1[:, b, :], ALU.add).then_inc(x1_done, 1)
            dve.wait_ge(x1_done, B)
            layer_norm(1, x1, xn)
            transposed_out(1, xnT)
            nc.vector.tensor_tensor(x1[:, :, :], x1[:, :, :], rb_a[:, :].unsqueeze(1).to_broadcast([P, B, D]), ALU.add).then_inc(bo2_added, 1)
            for n in range(2):
                dve.wait_ge(sp_mm, 3 + n)
                for o in range(2):
                    oc = 2 * n + o
                    i = nc.vector.tensor_scalar(k_s[:, oc, :], S[:, 2 + n, o * TOK:(o + 1) * TOK],
                                                bias_a[:, 1, oc:oc + 1], None, ALU.add)
                i.then_inc(sp_out, 1)
            dve.wait_ge(consts, 5)
            flat = S[:, :, :].rearrange("p g (c t) -> p (g c) t", c=IC)
            for b in range(B):
                dve.wait_ge(ss_mm, b + 1)
                if b > 0:
                    dve.wait_ge(sT_mm, 4 * b)
                nc.vector.tensor_tensor(sc_s[:, :, :], flat, causal[:, :].unsqueeze(1).to_broadcast([P, H, T]), ALU.add).then_inc(ss_masked, 1)
                dve.wait_ge(ss_masked, b + 1)
                nc.vector.tensor_reduce(smx[:, :], sc_s[:, :, :], AX.X, ALU.max).then_inc(ss_max, 1)
                dve.wait_ge(ss_max, b + 1)
                nc.vector.tensor_tensor(sc_s[:, :, :], sc_s[:, :, :], smx[:, :].unsqueeze(2).to_broadcast([P, H, T]),
                                        ALU.subtract).then_inc(ss_sub, 1)
                dve.wait_ge(ss_exp, b + 1)
                nc.vector.tensor_reduce(ssum[:, :], sc_s[:, :, :], AX.X, ALU.add).then_inc(ss_sum, 1)
                dve.wait_ge(ss_sum, b + 1)
                nc.vector.reciprocal(srd[:, :], ssum[:, :]).then_inc(ss_rd, 1)
                dve.wait_ge(ss_rd, b + 1)
                nc.vector.tensor_tensor(sc_s[:, :, :], sc_s[:, :, :], srd[:, :].unsqueeze(2).to_broadcast([P, H, T]),
                                        ALU.mult).then_inc(ss_normed, 1)
                for n in range(1, 4, 2):
                    dve.wait_ge(sT_mm, 4 * b + n + 1)
                    dve.wait_ge(sT_out, 4 * b + n)
                    nc.vector.tensor_copy(pt_s[:, 4 * n:4 * n + 4, :].rearrange("p h t -> p (h t)"), TP[:, 1, :]).then_inc(sT_out, 1)
                dve.wait_ge(so_mm, b + 1)
                for oc in range(IC):
                    i = nc.vector.tensor_scalar(a2T[:, oc, b * T:(b + 1) * T], TP[:, 2, oc * T:(oc + 1) * T],
                                                bias_a[:, 2, oc:oc + 1], None, ALU.add)
                i.then_inc(so_out, 1)
            dve.wait_ge(bo2_added, 1)
            for b in range(B):
                dve.wait_ge(oproj2_mm, b + 1)
                nc.vector.tensor_tensor(x1[:, b, :], S[:, b, :], x1[:, b, :], ALU.add).then_inc(x2_done, 1)
            dve.wait_ge(x2_done, B)
            layer_norm(2, x1, xn)
            transposed_out(2, xnT)
            for b in range(B):
                nc.vector.tensor_tensor(x3_lo[:, :, b * T:(b + 1) * T], TP[:, b, :].rearrange("p (c t) -> p c t", c=IC),
                                        f32(x3_hi[:, :, b * T:(b + 1) * T]), ALU.subtract).then_inc(x3_made, 1)

            def split_e(e, slot, k):
                dve.wait_ge(e_hi_made, 3 * e + k + 1)
                nc.vector.tensor_tensor(e_lo(slot)[:, k], eraw[:, k], f32(e_hi(slot)[:, k]), ALU.subtract).then_inc(e_made, 1)

            for k in range(3):
                split_e(0, 0, k)

            steps = [0]

            def step(i):
                steps[0] += 1
                i.then_inc(gate_step, 1)
                dve.wait_ge(gate_step, steps[0])

            dve.wait_ge(gate_mm, 1)
            for b in range(B):
                i = nc.vector.tensor_reduce(gsm[:, b, 0:1], TP[:, 2, b * E:(b + 1) * E], AX.X, ALU.max, negate=True)
            step(i)
            dve.wait_ge(gate_exp, B)
            step(nc.vector.memset(sc16[:, :, E:2 * E], -1.0))
            step(nc.vector.reciprocal(gsm[:, :, 2], gsm[:, :, 1]))
            for b in range(B):
                step(nc.vector.tensor_scalar(sc16[:, b, 0:E], sc16[:, b, 0:E], gsm[:, b, 2:3], None, ALU.mult))
                step(nc.vector.max(top8[:, b, :], sc16[:, b, 0:E]))
                step(nc.vector.memset(top8[:, b, 2:8], -1.0))
                step(nc.vector.match_replace(rep16[:, b, :], top8[:, b, :], sc16[:, b, :], 0.0))
                step(nc.vector.tensor_tensor(comb[:, b, 0:E], sc16[:, b, 0:E], rep16[:, b, 0:E], ALU.subtract))
                step(nc.vector.memset(comb[:, b, E:NE], 1.0))
            assert steps[0] == GATE_STEPS

            def second_biases():
                dve.wait_ge(combT_mm, 1)
                nc.vector.tensor_copy(combT[:, :], TP[0:NE, 2, 0:TOK]).then_inc(combT_out, 1)
                dve.wait_ge(b2_mm, 1)
                for b in range(B):
                    nc.vector.tensor_tensor(x1[:, b, :], S[:, B + b, :], x1[:, b, :], ALU.add).then_inc(acc_step, 1)

            def add_expert(e, slot):
                for b in range(B):
                    dve.wait_ge(y_mm, B * e + b + 1)
                    dve.wait_ge(acc_step, B * (e + 1))
                    nc.vector.scalar_tensor_tensor(x1[:, b, :], S[:, 2 * slot + b, :], comb[:, b, bass.ds(e, 1)],
                                                   x1[:, b, :], ALU.mult, ALU.add).then_inc(acc_step, 1)

            def expert(e, slot, first_one, last_one):
                for f in range(FC):
                    dve.wait_ge(silu_made, FC * e + f + 1)
                    nc.vector.scalar_tensor_tensor(gf[:, f % 2, :], TP[:, f % 2, TOK:2 * TOK], ebs[:, 1, bass.ds(e, 1), f],
                                                   silu[:, f % 2, :], ALU.add, ALU.mult).then_inc(g_made, 1)
                    dve.wait_ge(g_hi_made, FC * e + f + 1)
                    nc.vector.tensor_tensor(g_lo[:, slot, f, :], gf[:, f % 2, :], f32(g_hi[:, slot, f, :]),
                                            ALU.subtract).then_inc(g_split, 1)
                    if f < 3 and not last_one:
                        split_e(e + 1, 1 - slot, f)
                    if f == 1 and not first_one:
                        add_expert(e - 1, 1 - slot)
                if first_one:
                    second_biases()
                if last_one:
                    add_expert(e, slot)

            all_experts(dve, expert)


def kernel(**inputs):
    import numpy as np
    import concourse.bacc as bacc
    from concourse.bass_utils import run_bass_kernel_spmd

    a = {k: np.asarray(v) for k, v in inputs.items()}

    def rows(w):
        s = w.shape
        return np.swapaxes(w.reshape(s[:-2] + (IC, P, s[-1])), -3, -2)

    def cols(v):
        return np.moveaxis(v.reshape(v.shape[:-1] + (IC, P)), -1, 0)

    def lin(names):
        return np.stack([rows(a[n].T) for n in names])

    ctxT = a["ctx_1024"].reshape(B, NCH, CK, IC, P).transpose(0, 1, 4, 3, 2)
    x, f, s = "L0_xattn_", "L0_ffn_", "L0_attn_"

    def experts(n, m):
        return np.concatenate([a[f + n], a[f + m][None]])

    data = {
        "x": a["x"], "ctxT": ctxT, "mask": a["mask_BxS2_bf0"],
        "xwT": lin([x + "wq", x + "wk", x + "wv", x + "wo"]),
        "xbias": cols(np.stack([a[x + "bq"], a[x + "bk"], a[x + "bv"]])),
        "awT": lin([s + "Wq", s + "Wk", s + "Wv", s + "Wo"]),
        "abias": cols(np.stack([a[s + "bq"], a[s + "bk"], a[s + "bv"]])),
        "rowbias": np.stack([a[x + "bo"], a[s + "bo"]]),
        "gateT": rows(a[f + "gate_w"].T),
        "w1": rows(experts("w1", "sw1")), "w3": rows(experts("w3", "sw3")), "w2": rows(experts("w2", "sw2")),
        "eb": cols(np.stack([experts("b1", "sb1"), experts("b3", "sb3")])),
        "eb2": experts("b2", "sb2"),
    }
    nc = bacc.Bacc("TRN2", target_bir_lowering=False, num_devices=1)
    arrays, args = {}, []
    for name, v in data.items():
        v = np.ascontiguousarray(v)
        arrays[name] = v
        args.append(nc.dram_tensor(name, v.shape, mybir.dt.from_np(v.dtype), kind="ExternalInput").ap())
    args.append(nc.dram_tensor("out", (B, T, D), F32, kind="ExternalOutput").ap())
    perceiver_kernel(nc, *args)
    r = run_bass_kernel_spmd(nc, [arrays], core_ids=[0])
    return r.results[0]["out"]
```

```python
from contextlib import ExitStack

import concourse.bass as bass
from concourse import mybir

F32 = mybir.dt.float32
F32R = mybir.dt.float32r
U8 = mybir.dt.uint8
ALU = mybir.AluOpType
ACT = mybir.ActivationFunctionType
AX = mybir.AxisListType

P = 128
BANK = 512
B, T, D = 2, 128, 512
TOK = B * T
S2 = 2048
H, HD = 16, 32
IC = D // P
HPC = P // HD
SC = float(HD) ** -0.5
EPS = 1e-5
NEG = -1.0e30

STAGES = 2 * B
HS = H // 2
OC = HS // HPC
HW = OC * P
CK = 256
NCH = S2 // CK
KT = S2 // P
PAIRS = HS // 2
STEPS = KT // 2
STAGE_STEPS = PAIRS * STEPS
UNITS = 2 * HS
SCORES_AT = {0: 2, 1: 3, **{2 * (u - 3): u for u in range(4, UNITS)}}
EXP_AT = {1: 2, 2: 3, **{2 * (u - 3) + 2: u for u in range(4, UNITS)}}
FAC_AT = max(EXP_AT) + 1
LAG = 3
TB = 3
PTS = 3
PB = 4
KROWS = 3 * HD + 1

E = 8
NE = E + 1
GATE_STEPS = 3 + 6 * B
FC = 4


def perceiver_kernel(nc, x, ctxT, mask, xwT, xbias, awT, abias, rowbias, gateT,
                     w1, w3, w2, eb, eb2, out):
    q_dram = nc.dram_tensor("q_split", [2, P, IC, TOK], F32, kind="Internal").ap()
    mask_dram = nc.dram_tensor("mask_row", [B, S2], F32, kind="Internal").ap()

    ctx = ExitStack()
    with ctx:
        def sb(name, shape, dt=F32, scope=ctx):
            return scope.enter_context(nc.sbuf_tensor(name, shape, dt))

        def sem(name):
            return ctx.enter_context(nc.semaphore(name))

        ident = sb("ident", [P, P])
        bias_x = sb("bias_x", [P, 3, IC])
        bias_a = sb("bias_a", [P, 3, IC])
        aT = sb("aT", [P, IC, TOK])
        stat = sb("stat", [P, B, 6])
        mv = sb("mv", [P, B, 2])
        std = sb("std", [P, B])
        rstd = sb("rstd", [P, B])
        epsc = sb("epsc", [P, 1])

        proj = ExitStack()
        wraw = sb("wraw", [P, 2, IC, HW], F32, proj)
        w_hi = sb("w_hi", [P, 2, IC, HW], F32R, proj)
        w_lo = sb("w_lo", [P, 2, IC, HW], F32R, proj)
        proj.close()
        wo_x = sb("wo_x", [P, IC, D])
        swq = sb("swq", [P, IC, D])
        x1 = sb("x1", [P, B, D])
        rb_x = sb("rb_x", [P, D])
        rb_a = sb("rb_a", [P, D])

        att = ExitStack()
        craw = sb("craw", [P, 2, IC, CK], F32, att)
        c_hi = sb("c_hi", [P, 2, IC, CK], F32R, att)
        c_lo = sb("c_lo", [P, 2, IC, CK], F32R, att)
        qst = sb("qst", [P, OC, HPC, T], F32R, att)
        kst = sb("kst", [P, OC, HPC, S2], F32R, att)
        v_hi = sb("v_hi", [P, KT, HW], F32R, att)
        v_lo = sb("v_lo", [P, KT, HW], F32R, att)
        pt_hi = sb("pt_hi", [P, PB, BANK], F32R, att)
        pt_lo = sb("pt_lo", [P, PB, BANK], F32R, att)
        nmx = sb("nmx", [P, OC, 2, HPC], F32, att)
        den = sb("den", [P, OC, 2, HPC], F32, att)
        fac = sb("fac", [P, OC, 2, HPC], F32, att)
        nmin = sb("nmin", [P, OC, HPC], F32, att)
        dsum = sb("dsum", [P, OC, HPC], F32, att)
        oraw = sb("oraw", [P, OC, 2, T], F32, att)
        prob = sb("prob", [P, 4, S2], F32, att)
        k_parts = [prob[:, 2 + n, :].rearrange("p (l o k) -> p l o k", l=2, o=OC) for n in range(2)]
        fac_rep = prob[:, 0, 0:UNITS * HD].rearrange("p (u d) -> p u d", u=UNITS)
        x_a = prob[:, 0, 0:B * D].rearrange("p (b d) -> p b d", b=B)
        xn_a = prob[:, 0, B * D:2 * B * D].rearrange("p (b d) -> p b d", b=B)
        xnT_a = prob[:, 1, 0:IC * TOK].rearrange("p (c t) -> p c t", c=IC)
        wq_a = prob[:, 2, 0:IC * D].rearrange("p (c d) -> p c d", c=IC)
        mask_u = aT[0:B, :, :].rearrange("p c t -> p (c t)").bitcast(U8)[:, 0:S2]
        mask_r = v_lo[0:B, 0:S2 // HW, :].rearrange("p k d -> p (k d)")
        mask_nan = sb("mask_nan", [B, 2], F32, att)
        q_hi = kst[:, 0, 0, 0:IC * TOK].rearrange("p (c t) -> p c t", c=IC)
        q_lo = kst[:, 0, 1, 0:IC * TOK].rearrange("p (c t) -> p c t", c=IC)
        q_raw = prob[:, 3, 0:IC * TOK].rearrange("p (c t) -> p c t", c=IC)
        att.close()

        late = ExitStack()
        xn = sb("xn", [P, B, D], F32, late)
        xnT = sb("xnT", [P, IC, TOK], F32, late)
        x3_hi = sb("x3_hi", [P, IC, TOK], F32R, late)
        x3_lo = sb("x3_lo", [P, IC, TOK], F32R, late)
        gw = sb("gw", [P, IC, E], F32, late)
        ebs = sb("ebs", [P, 2, NE, FC], F32, late)
        b2s = sb("b2s", [NE, D], F32, late)
        sc16 = sb("sc16", [P, B, 2 * E], F32, late)
        rep16 = sb("rep16", [P, B, 2 * E], F32, late)
        top8 = sb("top8", [P, B, 8], F32, late)
        gsm = sb("gsm", [P, B, 4], F32, late)
        comb = sb("comb", [P, B, NE], F32, late)
        combT = sb("combT", [NE, TOK], F32, late)
        silu = sb("silu", [P, 2, TOK], F32, late)
        gf = sb("gf", [P, 2, TOK], F32, late)
        g_hi = sb("g_hi", [P, 2, FC, TOK], F32R, late)
        g_lo = sb("g_lo", [P, 2, FC, TOK], F32R, late)
        eraw = sb("eraw", [P, 3, IC, D], F32, late)
        e_hi0 = sb("e_hi0", [P, 3, IC, D], F32R, late)
        e_lo0 = sb("e_lo0", [P, 3, IC, D], F32R, late)
        self_ = ExitStack()
        swk = sb("swk", [P, IC, D], F32, self_)
        swv = sb("swv", [P, IC, D], F32, self_)
        swo = sb("swo", [P, IC, D], F32, self_)
        rb_v = sb("rb_v", [P, D], F32, self_)
        q_s = sb("q_s", [P, IC, TOK], F32, self_)
        k_s = sb("k_s", [P, IC, TOK], F32, self_)
        causal = sb("causal", [P, T], F32, self_)
        causal_r = sb("causal_r", [P, T], F32R, self_)
        ident_r = sb("ident_r", [P, P], F32R, self_)
        v_s = sb("v_s", [P, B, D], F32, self_)
        a2T = sb("a2T", [P, IC, TOK], F32, self_)
        sc_s = sb("sc_s", [P, B * HPC, IC, T], F32, self_)
        pt_s = sb("pt_s", [P, PTS, IC, T], F32, self_)
        snmx = sb("snmx", [P, B * HPC, IC], F32, self_)
        ssum = sb("ssum", [P, B * HPC, IC], F32, self_)
        srd = sb("srd", [P, B * HPC, IC], F32, self_)
        self_.close()
        e_hi1 = sb("e_hi1", [P, 3, IC, D], F32R, late)
        e_lo1 = sb("e_lo1", [P, 3, IC, D], F32R, late)
        late.close()

        S = ctx.enter_context(nc.psum_tensor("S", [P, 4, BANK], F32))
        TP = ctx.enter_context(nc.psum_tensor("TP", [P, TB, BANK], F32))
        O = ctx.enter_context(nc.psum_tensor("O", [P, BANK], F32))

        mask_in, x_in, wq_in, bias_in = sem("mask_in"), sem("x_in"), sem("wq_in"), sem("bias_in")
        consts = sem("consts")
        ones_made = sem("ones_made")
        mask_made, mask_stored = sem("mask_made"), sem("mask_stored")
        ln_stat, ln_mv, ln_std, ln_rstd, ln_done = (sem(n) for n in ("ln_stat", "ln_mv", "ln_std", "ln_rstd", "ln_done"))
        xT_mm, xT_out = sem("xT_mm"), sem("xT_out")
        q_mm, q_made, q_hi_out, q_lo_out, q_stored = sem("q_mm"), sem("q_made"), sem("q_hi_out"), sem("q_lo_out"), sem("q_stored")
        wraw_in = [sem("wraw_in_k"), sem("wraw_in_v")]
        craw_in = [sem("craw_in_0"), sem("craw_in_1")]
        w_hi_made, w_made = sem("w_hi_made"), sem("w_made")
        c_hi_made, c_made = sem("c_hi_made"), sem("c_made")
        k_mm, k_hi_out, k_out = sem("k_mm"), sem("k_hi_out"), sem("k_out")
        k_stacked = [[sem(f"k_stacked_{g}_{n}") for n in range(2)] for g in range(HPC)]
        v_mm, v_hi_out, v_out = sem("v_mm"), sem("v_hi_out"), sem("v_out")
        q_stacked = sem("q_stacked")
        s_mm, nmx_made, exp_done = sem("s_mm"), sem("nmx_made"), sem("exp_done")
        t_mm, pt_hi_out, pt_out, pv_mm, o_out = sem("t_mm"), sem("pt_hi_out"), sem("pt_out"), sem("pv_mm"), sem("o_out")
        fac_step, fac_exp, fac_made, rb_mm = sem("fac_step"), sem("fac_exp"), sem("fac_made"), sem("rb_mm")
        o_normed, a_done = sem("o_normed"), sem("a_done")
        late_w = [sem(f"late_w{i}") for i in range(5)]
        x1_in, row_in, rb_v_in, ffn_small_in = sem("x1_in"), sem("row_in"), sem("rb_v_in"), sem("ffn_small_in")
        bo_added, oproj_mm, x1_done = sem("bo_added"), sem("oproj_mm"), sem("x1_done")
        sp_mm = sem("sp_mm")
        sq_out, sk_out, sv_out, causal_made = sem("sq_out"), sem("sk_out"), sem("sv_out"), sem("causal_made")
        ss_mm, ss_max, ss_exp, ss_rd, ss_normed, sT_mm, sT_out = (
            sem(n) for n in ("ss_mm", "ss_max", "ss_exp", "ss_rd", "ss_normed", "sT_mm", "sT_out"))
        so_mm, so_out, bo2_added, oproj2_mm, x2_done = (sem(n) for n in ("so_mm", "so_out", "bo2_added", "oproj2_mm", "x2_done"))
        x3_hi_made, x3_made = sem("x3_hi_made"), sem("x3_made")
        gate_mm, gate_step, gate_exp, combT_mm, combT_out, b2_mm, acc_step = (
            sem(n) for n in ("gate_mm", "gate_step", "gate_exp", "combT_mm", "combT_out", "b2_mm", "acc_step"))
        eraw_in = [sem(f"eraw_in_{n}") for n in ("w1", "w3", "w2")]
        e_hi_made, e_made = sem("e_hi_made"), sem("e_made")
        h_mm, silu_made, g_made, g_hi_made, g_split, y_mm = (
            sem(n) for n in ("h_mm", "silu_made", "g_made", "g_hi_made", "g_split", "y_mm"))
        out_stored = sem("out_stored")

        KST = 3 * 16
        QST = (3 * HPC + 1) * 16
        PROJ = [x for c in range(NCH - 2) for x in (("K", c), ("V", c))] + [
            ("K", NCH - 2), ("K", NCH - 1), ("V", NCH - 2), ("V first half", NCH - 1), ("S", 0), ("S", 1), ("V", NCH - 1)]

        def unit(u):
            return 2 * (u // 4) + u % 2, u % 4 // 2

        def f32(ap):
            return ap.bitcast(F32)

        def all_stages(eng, first, stage):
            first()
            stage(0, False)
            with eng.Fori(1, STAGES - 1) as s:
                stage(s, False)
            stage(STAGES - 1, True)

        def all_experts(eng, expert):
            expert(0, 0, True, False)
            expert(1, 1, False, False)
            with eng.Fori(1, NE // 2) as k:
                expert(2 * k, 0, False, False)
                expert(2 * k + 1, 1, False, False)
            expert(NE - 1, 0, False, True)

        def e_hi(slot):
            return (e_hi0, e_hi1)[slot]

        def e_lo(slot):
            return (e_lo0, e_lo1)[slot]

        def up_bank(f):
            return TP[:, f, :] if f < 3 else O[:, :]

        block = ctx.enter_context(nc.Block())

        @block.sync
        def _(sp):
            def first():
                sp.dma_start(x_a, x.rearrange("b t d -> t b d")).then_inc(x_in, 16)
                sp.dma_start(wq_a, xwT[0]).then_inc(wq_in, 16)
                sp.dma_start(bias_x[:, :, :], xbias).then_inc(bias_in, 16)
                sp.dma_start(bias_a[:, :, :], abias).then_inc(bias_in, 16)
                sp.dma_start(mask_u, mask).then_inc(mask_in, 16)
                sp.wait_ge(mask_made, 5)
                sp.dma_start(mask_dram, f32(mask_r)).then_inc(mask_stored, 16)
                sp.wait_ge(q_lo_out, 2)
                sp.dma_start(q_dram[0], f32(q_hi)).then_inc(q_stored, 16)
                sp.dma_start(q_dram[1], f32(q_lo)).then_inc(q_stored, 16)
                sp.wait_ge(mask_stored, 16)
                sp.wait_ge(q_stored, 32)

            def stage(s, last):
                b, half = s // 2, s % 2
                for c in range(NCH):
                    if c == 0:
                        sp.wait_ge(s_mm, UNITS * s)
                        for g in range(HPC):
                            rows = slice(g * HD, (g + 1) * HD)
                            for at, part in ((0, 0), (HD, 0), (2 * HD, 1)):
                                sp.dma_start(f32(qst[at:at + HD, :, g, :]),
                                             q_dram[part][rows, bass.ds(half * OC, OC), bass.ds(b * T, T)]
                                             ).then_inc(q_stacked, 16)
                        sp.dma_start(f32(kst[3 * HD:KROWS, :, :, :]).rearrange("p o g k -> p (o g) k"),
                                     mask_dram[bass.ds(b, 1), :].unsqueeze(1).to_broadcast([1, HS, S2])
                                     ).then_inc(q_stacked, 16)
                    if c % 2:
                        sp.wait_ge(k_out, s * NCH + c + 1)
                        for g in range(HPC):
                            rows = slice(g * HD, (g + 1) * HD)
                            for at, part in ((0, 0), (HD, 1), (2 * HD, 0)):
                                sp.dma_start(f32(kst[at:at + HD, :, g, (c - 1) * CK:(c + 1) * CK]),
                                             k_parts[c // 2 % 2][rows, part]).then_inc(k_stacked[g][c // 2 % 2], 16)

            all_stages(sp, first, stage)

            sp.wait_ge(v_mm, STAGES * NCH)
            sp.dma_start(wo_x[:, :, :], xwT[3]).then_inc(late_w[0], 16)
            sp.dma_start(x1[:, :, :], x.rearrange("b t d -> t b d")).then_inc(x1_in, 16)
            sp.dma_start(rb_x[:, :], rowbias[0].partition_broadcast(P)).then_inc(row_in, 16)
            sp.dma_start(rb_a[:, :], rowbias[1].partition_broadcast(P)).then_inc(row_in, 16)
            sp.dma_start(swq[:, :, :], awT[0]).then_inc(late_w[1], 16)
            sp.wait_ge(a_done, STAGES * OC)
            for n, (w, src) in enumerate(((swk, awT[1]), (swv, awT[2]), (swo, awT[3]))):
                sp.dma_start(w[:, :, :], src).then_inc(late_w[2 + n], 16)
            sp.dma_start(rb_v[:, :], rowbias[2].partition_broadcast(P)).then_inc(rb_v_in, 16)

            def ffn_small():
                sp.dma_start(gw[:, :, :], gateT).then_inc(ffn_small_in, 16)
                sp.dma_start(ebs[:, :, :, :], eb).then_inc(ffn_small_in, 16)
                sp.dma_start(b2s[:, :], eb2).then_inc(ffn_small_in, 16)

            def expert(e, slot, first_one, last_one):
                for k, w in enumerate((w1, w3, w2)):
                    if not first_one:
                        sp.wait_ge(e_made, 3 * e + k - 2)
                    sp.dma_start(eraw[:, k], w[e] if isinstance(e, int) else w[bass.ds(e, 1)].rearrange(
                        "e p c d -> (e p) c d")).then_inc(eraw_in[k], 16)
                if first_one:
                    ffn_small()

            all_experts(sp, expert)
            sp.wait_ge(acc_step, B * (NE + 1))
            sp.dma_start(out.rearrange("b t d -> t b d"), x1[:, :, :]).then_inc(out_stored, 16)
            sp.wait_ge(out_stored, 16)

        @block.gpsimd
        def _(pool):
            nc.gpsimd.memset(ident[:, :], 0.0).then_inc(consts, 1)
            nc.gpsimd.memset(epsc[:, :], EPS).then_inc(consts, 1)
            pool.wait_ge(consts, 2)
            nc.gpsimd.affine_select(out=ident[:, :], in_=ident[:, :], compare_op=ALU.not_equal, fill=1.0,
                                    base=0, pattern=[[-1, P]], channel_multiplier=1).then_inc(consts, 1)
            pool.wait_ge(a_done, STAGES * OC)
            nc.gpsimd.memset(causal[:, :], 0.0).then_inc(consts, 1)
            pool.wait_ge(consts, 4)
            nc.gpsimd.affine_select(out=causal[:, :], in_=causal[:, :], compare_op=ALU.is_ge, fill=NEG,
                                    base=0, pattern=[[-1, T]], channel_multiplier=1).then_inc(consts, 1)
            for n in range(B * HPC):
                pool.wait_ge(ss_rd, n + 1)
                nc.gpsimd.tensor_tensor(sc_s[:, n], sc_s[:, n], srd[:, n, :].unsqueeze(2).to_broadcast([P, IC, T]),
                                        ALU.mult).then_inc(ss_normed, 1)

        @block.tensor
        def _(pe):
            def products(out_ap, a, b):
                for ic in range(IC):
                    (ah, al), (bh, bl) = a(ic), b(ic)
                    for n, (l, r) in enumerate(((ah, bh), (ah, bl), (al, bh))):
                        mm = nc.tensor.matmul(out_ap, l, r, start=(ic == 0 and n == 0),
                                              stop=(ic == IC - 1 and n == 2))
                return mm

            def plain(out_ap, a, b):
                for ic in range(IC):
                    mm = nc.tensor.matmul(out_ap, a(ic), b(ic), start=(ic == 0), stop=(ic == IC - 1))
                return mm

            def transpose_x(n, src):
                for b in range(B):
                    pe.wait_ge(ln_done, B * n + b + 1)
                    for ic in range(IC):
                        mm = nc.tensor.transpose(TP[:, b, ic * P:(ic + 1) * P], src[:, b, ic * P:(ic + 1) * P],
                                                 ident[:, :])
                    mm.then_inc(xT_mm, 1)

            def first():
                pe.wait_ge(consts, 3)
                pe.wait_ge(ones_made, 1)
                transpose_x(0, xn_a)
                pe.wait_ge(wq_in, 16)
                pe.wait_ge(xT_out, B)
                for oc in range(IC):
                    mm = plain(S[:, oc // 2, (oc % 2) * TOK:(oc % 2 + 1) * TOK],
                               lambda ic: wq_a[:, ic, oc * P:(oc + 1) * P], lambda ic: xnT_a[:, ic, :])
                    if oc % 2:
                        mm.then_inc(q_mm, 1)

            def project_k(s, c):
                if c == 0:
                    pe.wait_ge(w_made, 2 * s + 2)
                pe.wait_ge(c_made, s * NCH + c + 1)
                if c >= 2:
                    pe.wait_ge(k_out, s * NCH + c - 1)
                for o in range(OC):
                    cols = slice(o * P, (o + 1) * P)
                    mm = products(TP[:, c % 2, o * CK:(o + 1) * CK],
                                  lambda ic: (w_hi[:, 0, ic, cols], w_lo[:, 0, ic, cols]),
                                  lambda ic: (c_hi[:, c % 2, ic, :], c_lo[:, c % 2, ic, :]))
                mm.then_inc(k_mm, 1)

            def project_v(s, c, tiles):
                bank = TP[:, 2, :] if c % 2 == 0 else O[:, :]
                if c >= 2 and 0 in tiles:
                    pe.wait_ge(v_out, s * NCH + c - 1)
                if c == 1 and 0 in tiles:
                    pe.wait_ge(o_out, s * PAIRS)
                for k in tiles:
                    keys = slice(k * P, (k + 1) * P)
                    mm = products(bank[:, k * HW:(k + 1) * HW],
                                  lambda ic: (c_hi[:, c % 2, ic, keys], c_lo[:, c % 2, ic, keys]),
                                  lambda ic: (w_hi[:, 1, ic, :], w_lo[:, 1, ic, :]))
                if CK // P - 1 in tiles:
                    mm.then_inc(v_mm, 1)

            def scores(s, u):
                h, half = unit(u)
                if u == 0:
                    pe.wait_ge(q_stacked, QST * (s + 1))
                    pe.wait_ge(o_normed, s)
                if u in (0, 1, 4):
                    for g in (range(u, u + 1) if u < 4 else range(2, HPC)):
                        for n in range(2):
                            pe.wait_ge(k_stacked[g][n], KST * (NCH // 4) * (s + 1))
                if u >= 2:
                    pe.wait_ge(exp_done, UNITS * s + u - 1)
                for n in range(2):
                    keys = slice((2 * half + n) * BANK, (2 * half + n + 1) * BANK)
                    mm = nc.tensor.matmul(S[:, 2 * (u % 2) + n, :], qst[0:KROWS, h // HPC, h % HPC, :],
                                          kst[0:KROWS, h // HPC, h % HPC, keys], start=True, stop=True)
                mm.then_inc(s_mm, 1)

            def transposes(s, g):
                p, j = g // STEPS, g % STEPS
                if j % (STEPS // 2) == 0:
                    pe.wait_ge(exp_done, UNITS * s + 4 * p + 4 * j // STEPS + 2)
                if g >= TB:
                    pe.wait_ge(pt_out, s * STAGE_STEPS + g - TB + 1)
                elif g == 0:
                    pe.wait_ge(k_out, (s + 1) * NCH)
                elif g == 2:
                    pe.wait_ge(v_out, s * NCH + NCH - 1)
                for k in range(2):
                    for hl in range(2):
                        kt = 2 * j + k
                        mm = nc.tensor.transpose(TP[:, g % TB, (2 * k + hl) * P:(2 * k + hl + 1) * P],
                                                 prob[:, (2 * p + hl) % 4, kt * P:(kt + 1) * P], ident[:, :])
                mm.then_inc(t_mm, 1)

            def times_v(s, g):
                p, j = g // STEPS, g % STEPS
                pe.wait_ge(pt_out, s * STAGE_STEPS + g + 1)
                if g == 0:
                    pe.wait_ge(v_out, (s + 1) * NCH)
                elif j == 0:
                    pe.wait_ge(o_out, s * PAIRS + p)
                cols, half = slice((p // 2) * P, (p // 2 + 1) * P), j // (STEPS // 2)
                for k in range(2):
                    kt, pc = 2 * j + k, slice(k * 2 * P, (k + 1) * 2 * P)
                    for n, (l, r) in enumerate(((v_hi, pt_hi), (v_hi, pt_lo), (v_lo, pt_hi))):
                        mm = nc.tensor.matmul(O[:, half * 2 * P:(half + 1) * 2 * P], l[:, kt, cols], r[:, g % PB, pc],
                                              start=(kt % (KT // 2) == 0 and n == 0),
                                              stop=(kt % (KT // 2) == KT // 2 - 1 and n == 2))
                mm.then_inc(pv_mm, 1)

            def stage(s, last):
                for what, n in PROJ:
                    if what == "K":
                        project_k(s, n)
                    elif what == "V":
                        project_v(s, n, range(CK // P) if n < NCH - 1 else [1])
                    elif what == "V first half":
                        project_v(s, n, [0])
                    elif what == "S":
                        scores(s, n)
                for g in range(STAGE_STEPS + LAG):
                    if g < STAGE_STEPS:
                        if g in SCORES_AT:
                            scores(s, SCORES_AT[g])
                        transposes(s, g)
                    if g == STAGE_STEPS:
                        pe.wait_ge(fac_made, s + 1)
                        for n in range(2 * OC):
                            mm = nc.tensor.matmul(S[:, 0, n * P:(n + 1) * P],
                                                  fac_rep[:, n * HPC:(n + 1) * HPC, :].rearrange("p h d -> p (h d)"),
                                                  ident[:, :], start=True, stop=True)
                        mm.then_inc(rb_mm, 1)
                    if g >= LAG:
                        times_v(s, g - LAG)

            all_stages(pe, first, stage)

            for b in range(B):
                if b == 0:
                    pe.wait_ge(late_w[0], 16)
                    pe.wait_ge(a_done, STAGES // B * OC)
                else:
                    pe.wait_ge(a_done, STAGES * OC)
                plain(S[:, 1 + b, :], lambda ic: aT[:, ic, b * T:(b + 1) * T], lambda ic: wo_x[:, ic, :]).then_inc(oproj_mm, 1)
            transpose_x(1, xn)
            pe.wait_ge(xT_out, 2 * B)
            pe.wait_ge(x1_done, B)
            for n, w in enumerate((swq, swk)):
                pe.wait_ge(late_w[1 + n], 16)
                for oc in range(IC):
                    mm = plain(S[:, 2 * n + oc // 2, (oc % 2) * TOK:(oc % 2 + 1) * TOK],
                               lambda ic: w[:, ic, oc * P:(oc + 1) * P], lambda ic: xnT[:, ic, :])
                    if oc % 2:
                        mm.then_inc(sp_mm, 1)

            def self_v(b):
                pe.wait_ge(late_w[3], 16)
                plain(TP[:, b, :], lambda ic: xnT[:, ic, b * T:(b + 1) * T], lambda ic: swv[:, ic, :]).then_inc(sp_mm, 1)

            def self_scores(n):
                b, g = n // HPC, n % HPC
                if n == 0:
                    pe.wait_ge(sq_out, 2)
                    pe.wait_ge(sk_out, 2)
                    pe.wait_ge(causal_made, 2)
                elif n >= HPC:
                    pe.wait_ge(ss_exp, n - HPC + 1)
                nc.tensor.matmul(S[:, g, :], ident_r[:, :], causal_r[:, :].unsqueeze(1).to_broadcast([P, IC, T]),
                                 start=True, stop=False)
                for oc in range(IC):
                    mm = nc.tensor.matmul(S[:, g, oc * T:(oc + 1) * T],
                                          q_s[g * HD:(g + 1) * HD, oc, b * T:(b + 1) * T],
                                          k_s[g * HD:(g + 1) * HD, oc, b * T:(b + 1) * T],
                                          start=False, stop=(oc == IC - 1))
                mm.then_inc(ss_mm, 1)

            def self_transposes(n):
                pe.wait_ge(ss_normed, n + 1)
                if n < 2:
                    pe.wait_ge(sv_out, n + 1)
                else:
                    pe.wait_ge(sT_out, n - 1)
                for oc in range(IC):
                    mm = nc.tensor.transpose(TP[:, n % 2, oc * T:(oc + 1) * T], sc_s[:, n, oc, :], ident[:, :])
                mm.then_inc(sT_mm, 1)

            def self_times_v(n):
                b, g = n // HPC, n % HPC
                pe.wait_ge(sT_out, n + 1)
                out_bank = TP[:, 2, :] if b == 0 else O[:, :]
                for oc in range(IC):
                    h = HPC * oc + g
                    mm = nc.tensor.matmul(out_bank[g * HD:(g + 1) * HD, oc * T:(oc + 1) * T],
                                          v_s[:, b, h * HD:(h + 1) * HD], pt_s[:, n % PTS, oc, :], start=True, stop=True)
                mm.then_inc(so_mm, 1)

            def self_oproj(b):
                pe.wait_ge(late_w[4], 16)
                pe.wait_ge(so_out, b + 1)
                pe.wait_ge(ss_exp, HPC + b + 1)
                plain(S[:, b, :], lambda ic: a2T[:, ic, b * T:(b + 1) * T], lambda ic: swo[:, ic, :]).then_inc(oproj2_mm, 1)

            self_v(0)
            for n in range(HPC):
                self_scores(n)
            self_v(1)
            for n in range(B * HPC):
                self_transposes(n)
                if n + HPC < B * HPC:
                    self_scores(n + HPC)
                if n > 0:
                    self_times_v(n - 1)
                if n == B * HPC - 2:
                    self_oproj(0)
            self_times_v(B * HPC - 1)
            self_oproj(1)
            transpose_x(2, xn)
            pe.wait_ge(ffn_small_in, 48)
            pe.wait_ge(xT_out, 3 * B)
            for b in range(B):
                mm = plain(TP[:, 2, b * E:(b + 1) * E], lambda ic: xnT[:, ic, b * T:(b + 1) * T], lambda ic: gw[:, ic, :])
            mm.then_inc(gate_mm, 1)

            def second_biases():
                pe.wait_ge(gate_step, GATE_STEPS)
                for b in range(B):
                    mm = nc.tensor.transpose(S[0:NE, 0, b * T:(b + 1) * T], comb[:, b, :], ident[:, :])
                mm.then_inc(combT_mm, 1)
                pe.wait_ge(combT_out, 1)
                for b in range(B):
                    mm = nc.tensor.matmul(S[:, B + b, :], combT[:, b * T:(b + 1) * T], b2s[:, :], start=True, stop=True)
                mm.then_inc(b2_mm, 1)

            def up(e, slot, f):
                if f == 0:
                    pe.wait_ge(e_made, 3 * e + 2)
                if not isinstance(e, int) or e > 0:
                    pe.wait_ge(g_made, FC * (e - 1) + f + 1)
                elif f == 0:
                    pe.wait_ge(x3_made, B)
                elif f == 2:
                    pe.wait_ge(gate_exp, B)
                for n in range(2):
                    cols = slice(f * P, (f + 1) * P)
                    mm = products(up_bank(f)[:, n * TOK:(n + 1) * TOK],
                                  lambda ic: (e_hi(slot)[:, n, ic, cols], e_lo(slot)[:, n, ic, cols]),
                                  lambda ic: (x3_hi[:, ic, :], x3_lo[:, ic, :]))
                mm.then_inc(h_mm, 1)

            def down(e, slot):
                pe.wait_ge(g_split, FC * e + FC)
                pe.wait_ge(e_made, 3 * e + 3)
                pe.wait_ge(acc_step, B * e)
                for b in range(B):
                    mm = products(S[:, 2 * slot + b, :],
                                  lambda ic: (g_hi[:, slot, ic, b * T:(b + 1) * T], g_lo[:, slot, ic, b * T:(b + 1) * T]),
                                  lambda ic: (e_hi(slot)[:, 2, ic, :], e_lo(slot)[:, 2, ic, :]))
                    mm.then_inc(y_mm, 1)

            def expert(e, slot, first_one, last_one):
                for f in range(FC):
                    if f == 2 and not first_one:
                        down(e - 1, 1 - slot)
                    up(e, slot, f)
                if first_one:
                    second_biases()
                if last_one:
                    down(e, slot)

            all_experts(pe, expert)

        @block.scalar
        def _(act):
            def load_w(s):
                act.wait_ge(w_made, 2 * s)
                for n in range(2):
                    act.dma_start(wraw[:, n], xwT[1 + n][:, :, bass.ds((s % 2) * HW, HW)]).then_inc(wraw_in[n], 16)

            def load_c(s, c):
                act.dma_start(craw[:, c % 2], ctxT[s // 2, c]).then_inc(craw_in[c % 2], 16)

            def ln_sqrt(n, b):
                act.wait_ge(ln_mv, B * n + b + 1)
                nc.scalar.activation(std[:, b:b + 1], mv[:, b, 1:2], ACT.Sqrt, bias=epsc[:, 0:1]).then_inc(ln_std, 1)

            def split_w(s):
                for n in range(2):
                    act.wait_ge(wraw_in[n], 16 * s + 16)
                    nc.scalar.copy(w_hi[:, n], wraw[:, n]).then_inc(w_hi_made, 1)

            def split_c(s, c):
                act.wait_ge(craw_in[c % 2], 16 * (s * (NCH // 2) + c // 2 + 1))
                nc.scalar.copy(c_hi[:, c % 2], craw[:, c % 2]).then_inc(c_hi_made, 1)

            def first():
                load_w(0)
                load_c(0, 0)
                load_c(0, 1)
                act.wait_ge(consts, 2)
                for b in range(B):
                    ln_sqrt(0, b)
                for n in range(2):
                    act.wait_ge(q_made, n + 1)
                    nc.scalar.copy(q_hi[:, 2 * n:2 * n + 2, :], q_raw[:, 2 * n:2 * n + 2, :]).then_inc(q_hi_out, 1)
                split_w(0)
                split_c(0, 0)
                split_c(0, 1)

            def exps(s, u):
                h, half = unit(u)
                act.wait_ge(nmx_made, s * UNITS + u + 1)
                if u == 0:
                    act.wait_ge(t_mm, s * STAGE_STEPS)
                elif u >= 8:
                    act.wait_ge(t_mm, s * STAGE_STEPS + (u // 4 - 1) * STEPS)
                at = slice(half * 2 * BANK, (half + 1) * 2 * BANK)
                one = (slice(None), h // HPC, half, slice(h % HPC, h % HPC + 1))
                nc.scalar.activation(prob[:, h % 4, at], S[:, 2 * (u % 2):2 * (u % 2) + 2, :].rearrange("p n k -> p (n k)"),
                                     ACT.Exp, bias=nmx[one], accum_out=den[one]).then_inc(exp_done, 1)

            def stage(s, last):
                for what, n in PROJ:
                    if what == "K":
                        if n + 2 < NCH or not last:
                            act.wait_ge(c_made, s * NCH + n + 1)
                            load_c(s + (n + 2) // NCH, (n + 2) % NCH)
                        if n == 1 and not last:
                            load_w(s + 1)
                    elif what == "V":
                        act.wait_ge(v_mm, s * NCH + n + 1)
                        src = TP[:, 2, :] if n % 2 == 0 else O[:, :]
                        nc.scalar.copy(v_hi[:, 2 * n:2 * n + 2, :].rearrange("p k d -> p (k d)"), src).then_inc(v_hi_out, 1)
                        if n + 2 < NCH:
                            split_c(s, n + 2)
                    elif what == "S":
                        exps(s, n)
                for g in range(STAGE_STEPS):
                    p, j = g // STEPS, g % STEPS
                    act.wait_ge(t_mm, s * STAGE_STEPS + g + 1)
                    if g >= PB:
                        act.wait_ge(pv_mm, s * STAGE_STEPS + g - PB + 1)
                    nc.scalar.copy(pt_hi[:, g % PB, :], TP[:, g % TB, :]).then_inc(pt_hi_out, 1)
                    if g in EXP_AT:
                        exps(s, EXP_AT[g])
                    if g == FAC_AT + 1:
                        act.wait_ge(fac_step, 5 * s + 2)
                        nc.scalar.activation(fac[:, :, :, :], fac[:, :, :, :], ACT.Exp).then_inc(fac_exp, 1)
                    if g == STAGE_STEPS - 6 and not last:
                        split_w(s + 1)
                        split_c(s + 1, 0)
                    if g == STAGE_STEPS - 4 and not last:
                        split_c(s + 1, 1)

            all_stages(act, first, stage)

            for b in range(B):
                ln_sqrt(1, b)

            def split_e(e, slot, k):
                act.wait_ge(eraw_in[k], 16 * e + 16)
                if not isinstance(e, int) or e >= 2:
                    if k < 2:
                        act.wait_ge(h_mm, FC * (e - 1))
                    else:
                        act.wait_ge(y_mm, B * (e - 1))
                nc.scalar.copy(e_hi(slot)[:, k], eraw[:, k]).then_inc(e_hi_made, 1)

            act.wait_ge(consts, 5)
            nc.scalar.copy(causal_r[:, :], causal[:, :]).then_inc(causal_made, 1)
            nc.scalar.copy(ident_r[:, :], ident[:, :]).then_inc(causal_made, 1)
            for k in range(2):
                split_e(0, 0, k)
            for n in range(2):
                act.wait_ge(sp_mm, 3 + n)
                for o in range(2):
                    oc = 2 * n + o
                    i = nc.scalar.activation(k_s[:, oc, :], S[:, 2 + n, o * TOK:(o + 1) * TOK], ACT.Identity,
                                             bias=bias_a[:, 1, oc:oc + 1])
                i.then_inc(sk_out, 1)
            split_e(0, 0, 2)
            for n in range(B * HPC):
                act.wait_ge(ss_max, n + 1)
                for oc in range(IC):
                    i = nc.scalar.activation(sc_s[:, n, oc, :], S[:, n % HPC, oc * T:(oc + 1) * T], ACT.Exp,
                                             bias=snmx[:, n, oc:oc + 1], accum_out=ssum[:, n, oc:oc + 1])
                i.then_inc(ss_exp, 1)
            for b in range(B):
                ln_sqrt(2, b)

            for b in range(B):
                act.wait_ge(xT_mm, 2 * B + b + 1)
                nc.scalar.copy(x3_hi[:, :, b * T:(b + 1) * T], TP[:, b, :].rearrange("p (c t) -> p c t", c=IC)).then_inc(x3_hi_made, 1)
            act.wait_ge(gate_step, 1)
            for b in range(B):
                nc.scalar.activation(sc16[:, b, 0:E], TP[:, 2, b * E:(b + 1) * E], ACT.Exp,
                                     bias=gsm[:, b, 0:1], accum_out=gsm[:, b, 1:2]).then_inc(gate_exp, 1)

            def expert(e, slot, first_one, last_one):
                for f in range(FC):
                    act.wait_ge(h_mm, FC * e + f + 1)
                    act.wait_ge(ffn_small_in, 48)
                    nc.scalar.activation(silu[:, f % 2, :], up_bank(f)[:, 0:TOK], ACT.Silu,
                                         bias=ebs[:, 0, bass.ds(e, 1), f]).then_inc(silu_made, 1)
                    act.wait_ge(g_made, FC * e + f + 1)
                    if f == 0 and (not isinstance(e, int) or e >= 2):
                        act.wait_ge(y_mm, B * (e - 1))
                    nc.scalar.copy(g_hi[:, slot, f, :], gf[:, f % 2, :]).then_inc(g_hi_made, 1)
                    if f < 3 and not last_one:
                        split_e(e + 1, 1 - slot, f)

            all_experts(act, expert)

        @block.vector
        def _(dve):
            def layer_norm(n, b, src, dst):
                nc.vector.bn_stats(stat[:, b, :], src[:, b, :]).then_inc(ln_stat, 1)
                dve.wait_ge(ln_stat, B * n + b + 1)
                nc.vector.bn_aggr(mv[:, b, :], stat[:, b, :]).then_inc(ln_mv, 1)
                dve.wait_ge(ln_std, B * n + b + 1)
                nc.vector.reciprocal(rstd[:, b:b + 1], std[:, b:b + 1]).then_inc(ln_rstd, 1)
                dve.wait_ge(ln_rstd, B * n + b + 1)
                nc.vector.tensor_scalar(dst[:, b, :], src[:, b, :], mv[:, b, 0:1], rstd[:, b:b + 1],
                                        ALU.subtract, ALU.mult).then_inc(ln_done, 1)

            def transposed_out(n, dst):
                for b in range(B):
                    dve.wait_ge(xT_mm, B * n + b + 1)
                    if n == 2:
                        dve.wait_ge(x3_hi_made, b + 1)
                    nc.vector.tensor_copy(dst[:, :, b * T:(b + 1) * T],
                                          TP[:, b, :].rearrange("p (c t) -> p c t", c=IC)).then_inc(xT_out, 1)

            def split_w(s):
                for n in range(2):
                    dve.wait_ge(w_hi_made, 2 * s + n + 1)
                    nc.vector.tensor_tensor(w_lo[:, n], wraw[:, n], f32(w_hi[:, n]), ALU.subtract).then_inc(w_made, 1)

            def split_c(s, c):
                dve.wait_ge(c_hi_made, s * NCH + c + 1)
                nc.vector.tensor_tensor(c_lo[:, c % 2], craw[:, c % 2], f32(c_hi[:, c % 2]), ALU.subtract).then_inc(c_made, 1)

            def first():
                nc.vector.memset(f32(qst[3 * HD:KROWS, :, :, :]), 1.0).then_inc(ones_made, 1)
                dve.wait_ge(x_in, 16)
                for b in range(B):
                    layer_norm(0, b, x_a, xn_a)
                transposed_out(0, xnT_a)
                dve.wait_ge(mask_in, 16)
                nc.vector.tensor_reduce(mask_nan[:, 0:1], mask_u, AX.X, ALU.min).then_inc(mask_made, 1)
                dve.wait_ge(mask_made, 1)
                nc.vector.tensor_scalar(mask_nan[:, 0:1], mask_nan[:, 0:1], -3.0e38, 10.0, ALU.mult, ALU.mult).then_inc(mask_made, 1)
                dve.wait_ge(mask_made, 2)
                nc.vector.tensor_tensor(mask_nan[:, 1:2], mask_nan[:, 0:1], mask_nan[:, 0:1], ALU.subtract).then_inc(mask_made, 1)
                dve.wait_ge(mask_made, 3)
                nc.vector.tensor_scalar(mask_r, mask_u, NEG, mask_nan[:, 1:2], ALU.mult, ALU.add).then_inc(mask_made, 2)
                dve.wait_ge(bias_in, 32)
                for n in range(2):
                    dve.wait_ge(q_mm, n + 1)
                    for o in range(2):
                        oc = 2 * n + o
                        i = nc.vector.tensor_scalar(q_raw[:, oc, :], S[:, n, o * TOK:(o + 1) * TOK],
                                                    bias_x[:, 0, oc:oc + 1], SC, ALU.add, ALU.mult)
                    i.then_inc(q_made, 1)
                for n in range(2):
                    dve.wait_ge(q_hi_out, n + 1)
                    nc.vector.tensor_tensor(q_lo[:, 2 * n:2 * n + 2, :], q_raw[:, 2 * n:2 * n + 2, :],
                                            f32(q_hi[:, 2 * n:2 * n + 2, :]), ALU.subtract).then_inc(q_lo_out, 1)
                split_w(0)
                split_c(0, 0)
                split_c(0, 1)
                dve.wait_ge(mask_stored, 16)

            def maximum(s, u):
                h, half = unit(u)
                if u == 0:
                    dve.wait_ge(exp_done, UNITS * s)
                dve.wait_ge(s_mm, s * UNITS + u + 1)
                nc.vector.tensor_reduce(nmx[:, h // HPC, half, h % HPC:h % HPC + 1],
                                        S[:, 2 * (u % 2):2 * (u % 2) + 2, :].rearrange("p n k -> p (n k)"),
                                        AX.X, ALU.max, negate=True).then_inc(nmx_made, 1)

            def outputs_out(s, p):
                dve.wait_ge(pv_mm, s * STAGE_STEPS + (p + 1) * STEPS)
                if p == 0:
                    dve.wait_ge(o_normed, s)
                for hl in range(2):
                    g = (2 * p + hl) % HPC
                    i = nc.vector.tensor_copy(oraw[g * HD:(g + 1) * HD, p // 2, :, :],
                                              O[g * HD:(g + 1) * HD, :].rearrange("p (i l t) -> p i l t", i=2, l=2)[:, :, hl, :])
                i.then_inc(o_out, 1)

            def factors_start(s):
                dve.wait_ge(exp_done, UNITS * (s + 1))
                nc.vector.tensor_tensor(nmin[:, :, :], nmx[:, :, 0, :], nmx[:, :, 1, :], ALU.min).then_inc(fac_step, 1)
                dve.wait_ge(fac_step, 5 * s + 1)
                nc.vector.tensor_tensor(fac[:, :, :, :], nmin[:, :, :].unsqueeze(2).to_broadcast([P, OC, 2, HPC]),
                                        nmx[:, :, :, :], ALU.subtract).then_inc(fac_step, 1)

            def factors_end(s):
                dve.wait_ge(fac_exp, s + 1)
                nc.vector.tensor_tensor(den[:, :, :, :], den[:, :, :, :], fac[:, :, :, :], ALU.mult).then_inc(fac_step, 1)
                dve.wait_ge(fac_step, 5 * s + 3)
                nc.vector.tensor_tensor(dsum[:, :, :], den[:, :, 0, :], den[:, :, 1, :], ALU.add).then_inc(fac_step, 1)
                dve.wait_ge(fac_step, 5 * s + 4)
                nc.vector.reciprocal(nmin[:, :, :], dsum[:, :, :]).then_inc(fac_step, 1)
                dve.wait_ge(fac_step, 5 * s + 5)
                dve.wait_ge(t_mm, s * STAGE_STEPS + (PAIRS - 1) * STEPS)
                for o in range(OC):
                    for i in range(2):
                        n = (2 * o + i) * HPC
                        f = nc.vector.tensor_tensor(fac_rep[:, n:n + HPC, :],
                                                    fac[:, o, i, :].unsqueeze(2).to_broadcast([P, HPC, HD]),
                                                    nmin[:, o, :].unsqueeze(2).to_broadcast([P, HPC, HD]), ALU.mult)
                f.then_inc(fac_made, 1)

            def stage(s, last):
                for what, n in PROJ:
                    if what == "K":
                        dve.wait_ge(k_mm, s * NCH + n + 1)
                        part = [k_parts[n // 2 % 2][:, l, :, (n % 2) * CK:(n % 2 + 1) * CK] for l in range(2)]
                        if n % 2 == 0 and n >= 4:
                            for g in range(HPC):
                                dve.wait_ge(k_stacked[g][n // 2 % 2], KST * (s * (NCH // 4) + n // 4))
                        elif n == 0:
                            dve.wait_ge(t_mm, s * STAGE_STEPS)
                            dve.wait_ge(q_stored, 32)
                        for o in range(OC):
                            i = nc.vector.tensor_scalar(part[0][:, o].bitcast(F32R), TP[:, n % 2, o * CK:(o + 1) * CK],
                                                        bias_x[:, 1, bass.ds((s % 2) * OC + o, 1)], None, ALU.add)
                        i.then_inc(k_hi_out, 1)
                        dve.wait_ge(k_hi_out, s * NCH + n + 1)
                        for o in range(OC):
                            i = nc.vector.scalar_tensor_tensor(part[1][:, o].bitcast(F32R), TP[:, n % 2, o * CK:(o + 1) * CK],
                                                               bias_x[:, 1, bass.ds((s % 2) * OC + o, 1)],
                                                               part[0][:, o], ALU.add, ALU.subtract)
                        i.then_inc(k_out, 1)
                    elif what == "V":
                        dve.wait_ge(v_hi_out, s * NCH + n + 1)
                        src = TP[:, 2, :] if n % 2 == 0 else O[:, :]
                        nc.vector.tensor_tensor(v_lo[:, 2 * n:2 * n + 2, :].rearrange("p k d -> p (k d)"), src,
                                                f32(v_hi[:, 2 * n:2 * n + 2, :]).rearrange("p k d -> p (k d)"),
                                                ALU.subtract).then_inc(v_out, 1)
                        if n + 2 < NCH:
                            split_c(s, n + 2)
                    elif what == "S":
                        maximum(s, n)
                for g in range(STAGE_STEPS):
                    p, j = g // STEPS, g % STEPS
                    dve.wait_ge(pt_hi_out, s * STAGE_STEPS + g + 1)
                    nc.vector.tensor_tensor(pt_lo[:, g % PB, :], TP[:, g % TB, :], f32(pt_hi[:, g % PB, :]),
                                            ALU.subtract).then_inc(pt_out, 1)
                    if j == LAG - 1 and p > 0:
                        outputs_out(s, p - 1)
                    if g in SCORES_AT:
                        maximum(s, SCORES_AT[g])
                    if g == FAC_AT:
                        factors_start(s)
                    if g == FAC_AT + 1:
                        factors_end(s)
                    if g == STAGE_STEPS - 6 and not last:
                        split_w(s + 1)
                        split_c(s + 1, 0)
                    if g == STAGE_STEPS - 4 and not last:
                        split_c(s + 1, 1)
                outputs_out(s, PAIRS - 1)
                dve.wait_ge(rb_mm, s + 1)
                dve.wait_ge(o_out, (s + 1) * PAIRS)
                nc.vector.tensor_tensor(oraw[:, :, :, :].rearrange("p o i t -> p (o i t)"), S[:, 0, :],
                                        oraw[:, :, :, :].rearrange("p o i t -> p (o i t)"), ALU.mult).then_inc(o_normed, 1)
                dve.wait_ge(o_normed, s + 1)
                for o in range(OC):
                    nc.vector.scalar_tensor_tensor(aT[:, bass.ds((s % 2) * OC + o, 1), bass.ds((s // 2) * T, T)],
                                                   oraw[:, o:o + 1, 0, :], bias_x[:, 2, bass.ds((s % 2) * OC + o, 1)],
                                                   oraw[:, o:o + 1, 1, :], ALU.add, ALU.add).then_inc(a_done, 1)

            all_stages(dve, first, stage)

            dve.wait_ge(x1_in, 16)
            dve.wait_ge(row_in, 32)
            nc.vector.tensor_tensor(x1[:, :, :], x1[:, :, :], rb_x[:, :].unsqueeze(1).to_broadcast([P, B, D]), ALU.add).then_inc(bo_added, 1)
            dve.wait_ge(bo_added, 1)
            for b in range(B):
                dve.wait_ge(oproj_mm, b + 1)
                nc.vector.tensor_tensor(x1[:, b, :], S[:, 1 + b, :], x1[:, b, :], ALU.add).then_inc(x1_done, 1)
                dve.wait_ge(x1_done, b + 1)
                layer_norm(1, b, x1, xn)
            transposed_out(1, xnT)
            nc.vector.tensor_tensor(x1[:, :, :], x1[:, :, :], rb_a[:, :].unsqueeze(1).to_broadcast([P, B, D]), ALU.add).then_inc(bo2_added, 1)

            def split_e(e, slot, k):
                dve.wait_ge(e_hi_made, 3 * e + k + 1)
                nc.vector.tensor_tensor(e_lo(slot)[:, k], eraw[:, k], f32(e_hi(slot)[:, k]), ALU.subtract).then_inc(e_made, 1)

            split_e(0, 0, 0)
            for n in range(2):
                dve.wait_ge(sp_mm, 1 + n)
                for o in range(2):
                    oc = 2 * n + o
                    i = nc.vector.tensor_scalar(q_s[:, oc, :], S[:, n, o * TOK:(o + 1) * TOK],
                                                bias_a[:, 0, oc:oc + 1], SC, ALU.add, ALU.mult)
                i.then_inc(sq_out, 1)
            split_e(0, 0, 1)

            def self_v(b):
                if b == 0:
                    dve.wait_ge(rb_v_in, 16)
                dve.wait_ge(sp_mm, 5 + b)
                nc.vector.tensor_tensor(v_s[:, b, :], TP[:, b, :], rb_v[:, :], ALU.add).then_inc(sv_out, 1)

            def self_max(n):
                dve.wait_ge(ss_mm, n + 1)
                nc.vector.tensor_reduce(snmx[:, n, :], S[:, n % HPC, :].rearrange("p (c t) -> p c t", c=IC), AX.X,
                                        ALU.max, negate=True).then_inc(ss_max, 1)

            def self_rd(n):
                dve.wait_ge(ss_exp, n + 1)
                nc.vector.reciprocal(srd[:, n, :], ssum[:, n, :]).then_inc(ss_rd, 1)

            def self_pt(n):
                dve.wait_ge(sT_mm, n + 1)
                if n >= PTS:
                    dve.wait_ge(so_mm, n - PTS + 1)
                nc.vector.tensor_copy(pt_s[:, n % PTS].rearrange("p c t -> p (c t)"), TP[:, n % 2, :]).then_inc(sT_out, 1)
                if n % HPC == HPC - 1:
                    b = n // HPC
                    dve.wait_ge(so_mm, HPC * (b + 1))
                    nc.vector.tensor_copy(a2T[:, :, b * T:(b + 1) * T],
                                          (TP[:, 2, :] if b == 0 else O[:, :]).rearrange("p (c t) -> p c t", c=IC)).then_inc(so_out, 1)

            self_v(0)
            for n in range(B * HPC + 3):
                if n < B * HPC:
                    self_max(n)
                if n == 1:
                    self_v(1)
                if 1 <= n <= B * HPC:
                    self_rd(n - 1)
                if n >= 3:
                    self_pt(n - 3)
            split_e(0, 0, 2)
            dve.wait_ge(bo2_added, 1)
            for b in range(B):
                dve.wait_ge(oproj2_mm, b + 1)
                nc.vector.tensor_tensor(x1[:, b, :], S[:, b, :], x1[:, b, :], ALU.add).then_inc(x2_done, 1)
                dve.wait_ge(x2_done, b + 1)
                layer_norm(2, b, x1, xn)
            transposed_out(2, xnT)
            for b in range(B):
                nc.vector.tensor_tensor(x3_lo[:, :, b * T:(b + 1) * T], TP[:, b, :].rearrange("p (c t) -> p c t", c=IC),
                                        f32(x3_hi[:, :, b * T:(b + 1) * T]), ALU.subtract).then_inc(x3_made, 1)

            steps = [0]

            def step(i):
                steps[0] += 1
                i.then_inc(gate_step, 1)
                dve.wait_ge(gate_step, steps[0])

            dve.wait_ge(gate_mm, 1)
            for b in range(B):
                i = nc.vector.tensor_reduce(gsm[:, b, 0:1], TP[:, 2, b * E:(b + 1) * E], AX.X, ALU.max, negate=True)
            step(i)
            dve.wait_ge(gate_exp, B)
            step(nc.vector.memset(sc16[:, :, E:2 * E], -1.0))
            step(nc.vector.reciprocal(gsm[:, :, 2], gsm[:, :, 1]))
            for b in range(B):
                step(nc.vector.tensor_scalar(sc16[:, b, 0:E], sc16[:, b, 0:E], gsm[:, b, 2:3], None, ALU.mult))
                step(nc.vector.max(top8[:, b, :], sc16[:, b, 0:E]))
                step(nc.vector.memset(top8[:, b, 2:8], -1.0))
                step(nc.vector.match_replace(rep16[:, b, :], top8[:, b, :], sc16[:, b, :], 0.0))
                step(nc.vector.tensor_tensor(comb[:, b, 0:E], sc16[:, b, 0:E], rep16[:, b, 0:E], ALU.subtract))
                step(nc.vector.memset(comb[:, b, E:NE], 1.0))
            assert steps[0] == GATE_STEPS

            def second_biases():
                dve.wait_ge(combT_mm, 1)
                nc.vector.tensor_copy(combT[:, :], S[0:NE, 0, 0:TOK]).then_inc(combT_out, 1)
                dve.wait_ge(b2_mm, 1)
                for b in range(B):
                    nc.vector.tensor_tensor(x1[:, b, :], S[:, B + b, :], x1[:, b, :], ALU.add).then_inc(acc_step, 1)

            def add_expert(e, slot):
                for b in range(B):
                    dve.wait_ge(y_mm, B * e + b + 1)
                    dve.wait_ge(acc_step, B * (e + 1))
                    nc.vector.scalar_tensor_tensor(x1[:, b, :], S[:, 2 * slot + b, :], comb[:, b, bass.ds(e, 1)],
                                                   x1[:, b, :], ALU.mult, ALU.add).then_inc(acc_step, 1)

            def expert(e, slot, first_one, last_one):
                for f in range(FC):
                    dve.wait_ge(silu_made, FC * e + f + 1)
                    nc.vector.scalar_tensor_tensor(gf[:, f % 2, :], up_bank(f)[:, TOK:2 * TOK], ebs[:, 1, bass.ds(e, 1), f],
                                                   silu[:, f % 2, :], ALU.add, ALU.mult).then_inc(g_made, 1)
                    dve.wait_ge(g_hi_made, FC * e + f + 1)
                    nc.vector.tensor_tensor(g_lo[:, slot, f, :], gf[:, f % 2, :], f32(g_hi[:, slot, f, :]),
                                            ALU.subtract).then_inc(g_split, 1)
                    if f == 2 and not first_one:
                        add_expert(e - 1, 1 - slot)
                    if f < 3 and not last_one:
                        split_e(e + 1, 1 - slot, f)
                if first_one:
                    second_biases()
                if last_one:
                    add_expert(e, slot)

            all_experts(dve, expert)


def kernel(**inputs):
    import numpy as np
    import concourse.bacc as bacc
    from concourse.bass_utils import run_bass_kernel_spmd

    a = {k: np.asarray(v) for k, v in inputs.items()}

    def rows(w):
        s = w.shape
        return np.swapaxes(w.reshape(s[:-2] + (IC, P, s[-1])), -3, -2)

    def cols(v):
        return np.moveaxis(v.reshape(v.shape[:-1] + (IC, P)), -1, 0)

    def lin(names):
        return np.stack([rows(a[n].T) for n in names])

    ctxT = a["ctx_1024"].reshape(B, NCH, CK, IC, P).transpose(0, 1, 4, 3, 2)
    x, f, s = "L0_xattn_", "L0_ffn_", "L0_attn_"

    def experts(n, m):
        return np.concatenate([a[f + n], a[f + m][None]])

    data = {
        "x": a["x"], "ctxT": ctxT, "mask": a["mask_BxS2_bf0"],
        "xwT": lin([x + "wq", x + "wk", x + "wv", x + "wo"]),
        "xbias": cols(np.stack([a[x + "bq"], a[x + "bk"], a[x + "bv"]])),
        "awT": lin([s + "Wq", s + "Wk", s + "Wv", s + "Wo"]),
        "abias": cols(np.stack([a[s + "bq"], a[s + "bk"], a[s + "bv"]])),
        "rowbias": np.stack([a[x + "bo"], a[s + "bo"], a[s + "bv"]]),
        "gateT": rows(a[f + "gate_w"].T),
        "w1": rows(experts("w1", "sw1")), "w3": rows(experts("w3", "sw3")), "w2": rows(experts("w2", "sw2")),
        "eb": cols(np.stack([experts("b1", "sb1"), experts("b3", "sb3")])),
        "eb2": experts("b2", "sb2"),
    }
    nc = bacc.Bacc("TRN2", target_bir_lowering=False, num_devices=1)
    arrays, args = {}, []
    for name, v in data.items():
        v = np.ascontiguousarray(v)
        arrays[name] = v
        args.append(nc.dram_tensor(name, v.shape, mybir.dt.from_np(v.dtype), kind="ExternalInput").ap())
    args.append(nc.dram_tensor("out", (B, T, D), F32, kind="ExternalOutput").ap())
    perceiver_kernel(nc, *args)
    r = run_bass_kernel_spmd(nc, [arrays], core_ids=[0])
    return r.results[0]["out"]
```

```python
from contextlib import ExitStack

import concourse.bass as bass
from concourse import mybir

F32 = mybir.dt.float32
F32R = mybir.dt.float32r
U8 = mybir.dt.uint8
ALU = mybir.AluOpType
ACT = mybir.ActivationFunctionType
AX = mybir.AxisListType

P = 128
BANK = 512
B, T, D = 2, 128, 512
TOK = B * T
S2 = 2048
H, HD = 16, 32
IC = D // P
HPC = P // HD
SC = float(HD) ** -0.5
EPS = 1e-5
NEG = -1.0e30

STAGES = 2 * B
HS = H // 2
OC = HS // HPC
HW = OC * P
CK = 256
NCH = S2 // CK
KT = S2 // P
PAIRS = HS // 2
STEPS = KT // 2
STAGE_STEPS = PAIRS * STEPS
UNITS = 2 * HS
SCORES_AT = {0: 2, 1: 3, 3: 4, **{2 * (u - 3): u for u in range(5, UNITS)}}
EXP_AT = {1: 2, 2: 3, **{2 * (u - 3) + 2: u for u in range(4, UNITS)}}
SPLIT_W_AT = {27: 0, 28: 1}
SPLIT_C_AT = {29: 0, 31: 1}
FAC_AT = max(EXP_AT) + 1
LAG = 3
TB = 3
PTS = 3
PB = 4
KROWS = 3 * HD + 1

E = 8
NE = E + 1
GATE_STEPS = 3 + 6 * B
FC = 4


def perceiver_kernel(nc, x, ctxT, mask, xwT, xbias, awT, abias, rowbias, gateT,
                     w1, w3, w2, eb, eb2, out):
    q_dram = nc.dram_tensor("q_stack", [3 * HD, IC, HPC, TOK], F32, kind="Internal").ap()
    mask_dram = nc.dram_tensor("mask_row", [B, S2], F32, kind="Internal").ap()

    ctx = ExitStack()
    with ctx:
        def sb(name, shape, dt=F32, scope=ctx):
            return scope.enter_context(nc.sbuf_tensor(name, shape, dt))

        def sem(name):
            return ctx.enter_context(nc.semaphore(name))

        ident = sb("ident", [P, P])
        bias_x = sb("bias_x", [P, 3, IC])
        bias_a = sb("bias_a", [P, 3, IC])
        aT = sb("aT", [P, IC, TOK])
        stat = sb("stat", [P, B, 6])
        mv = sb("mv", [P, B, 2])
        std = sb("std", [P, B])
        rstd = sb("rstd", [P, B])
        epsc = sb("epsc", [P, 1])
        fold = sb("fold", [P, 2, P])

        proj = ExitStack()
        wraw = sb("wraw", [P, 2, IC, HW], F32, proj)
        w_hi = sb("w_hi", [P, 2, IC, HW], F32R, proj)
        w_lo = sb("w_lo", [P, 2, IC, HW], F32R, proj)
        proj.close()
        wo_x = sb("wo_x", [P, IC, D])
        swq = sb("swq", [P, IC, D])
        x1 = sb("x1", [P, B, D])
        rb_x = sb("rb_x", [P, D])
        rb_a = sb("rb_a", [P, D])

        att = ExitStack()
        craw = sb("craw", [P, 2, IC, CK], F32, att)
        c_hi = sb("c_hi", [P, 2, IC, CK], F32R, att)
        c_lo = sb("c_lo", [P, 2, IC, CK], F32R, att)
        qst = sb("qst", [P, OC, HPC, T], F32R, att)
        kst = sb("kst", [P, OC, HPC, S2], F32R, att)
        v_pk = sb("v_pk", [P, KT, HS, 2, HD], F32R, att)
        pt_hi = sb("pt_hi", [P, PB, BANK], F32R, att)
        pt_lo = sb("pt_lo", [P, PB, BANK], F32R, att)
        nmx = sb("nmx", [P, OC, 2, HPC], F32, att)
        den = sb("den", [P, OC, 2, HPC], F32, att)
        fac = sb("fac", [P, OC, 2, HPC], F32, att)
        nmin = sb("nmin", [P, OC, HPC], F32, att)
        dsum = sb("dsum", [P, OC, HPC], F32, att)
        oraw = sb("oraw", [P, PAIRS, 2, T], F32, att)
        prob = sb("prob", [P, 4, S2], F32, att)
        k_parts = [prob[:, 2 + n, :].rearrange("p (l o k) -> p l o k", l=2, o=OC) for n in range(2)]
        fac_rep = prob[:, 0, 0:2 * UNITS * HD].rearrange("p (a i l d) -> p a i l d", a=PAIRS, i=2, l=2)
        x_a = prob[:, 0, 0:B * D].rearrange("p (b d) -> p b d", b=B)
        xn_a = prob[:, 0, B * D:2 * B * D].rearrange("p (b d) -> p b d", b=B)
        xnT_a = prob[:, 1, 0:IC * TOK].rearrange("p (c t) -> p c t", c=IC)
        wq_a = prob[:, 2, 0:IC * D].rearrange("p (c d) -> p c d", c=IC)
        mask_u = aT[0:B, :, :].rearrange("p c t -> p (c t)").bitcast(U8)[:, 0:S2]
        mask_r = v_pk[0:B, 0:S2 // (2 * HW), :, :, :].rearrange("p k h n d -> p (k h n d)")
        mask_nan = sb("mask_nan", [B, 2], F32, att)
        q_hi = kst[:, 0, 0, 0:IC * TOK].rearrange("p (c t) -> p c t", c=IC)
        q_lo = kst[:, 0, 1, 0:IC * TOK].rearrange("p (c t) -> p c t", c=IC)
        q_raw = prob[:, 3, 0:IC * TOK].rearrange("p (c t) -> p c t", c=IC)
        att.close()

        late = ExitStack()
        xn = sb("xn", [P, B, D], F32, late)
        xnT = sb("xnT", [P, IC, TOK], F32, late)
        x3_hi = sb("x3_hi", [P, IC, TOK], F32R, late)
        x3_lo = sb("x3_lo", [P, IC, TOK], F32R, late)
        gw = sb("gw", [P, IC, E], F32, late)
        ebs = sb("ebs", [P, 2, NE, FC], F32, late)
        b2s = sb("b2s", [NE, D], F32, late)
        sc16 = sb("sc16", [P, B, 2 * E], F32, late)
        rep16 = sb("rep16", [P, B, 2 * E], F32, late)
        top8 = sb("top8", [P, B, 8], F32, late)
        gsm = sb("gsm", [P, B, 4], F32, late)
        comb = sb("comb", [P, B, NE], F32, late)
        combT = sb("combT", [NE, TOK], F32, late)
        silu = sb("silu", [P, 2, TOK], F32, late)
        gf = sb("gf", [P, 2, TOK], F32, late)
        g_hi = sb("g_hi", [P, 2, FC, TOK], F32R, late)
        g_lo = sb("g_lo", [P, 2, FC, TOK], F32R, late)
        eraw = sb("eraw", [P, 3, IC, D], F32, late)
        e_hi0 = sb("e_hi0", [P, 3, IC, D], F32R, late)
        e_lo0 = sb("e_lo0", [P, 3, IC, D], F32R, late)
        self_ = ExitStack()
        swk = sb("swk", [P, IC, D], F32, self_)
        swv = sb("swv", [P, IC, D], F32, self_)
        swo = sb("swo", [P, IC, D], F32, self_)
        rb_v = sb("rb_v", [P, D], F32, self_)
        q_s = sb("q_s", [P, IC, TOK], F32, self_)
        k_s = sb("k_s", [P, IC, TOK], F32, self_)
        causal = sb("causal", [P, T], F32, self_)
        causal_r = sb("causal_r", [P, T], F32R, self_)
        ident_r = sb("ident_r", [P, P], F32R, self_)
        v_s = sb("v_s", [P, B, D], F32, self_)
        a2T = sb("a2T", [P, IC, TOK], F32, self_)
        sc_s = sb("sc_s", [P, B * HPC, IC, T], F32, self_)
        pt_s = sb("pt_s", [P, PTS, IC, T], F32, self_)
        snmx = sb("snmx", [P, B * HPC, IC], F32, self_)
        ssum = sb("ssum", [P, B * HPC, IC], F32, self_)
        srd = sb("srd", [P, B * HPC, IC], F32, self_)
        self_.close()
        e_hi1 = sb("e_hi1", [P, 3, IC, D], F32R, late)
        e_lo1 = sb("e_lo1", [P, 3, IC, D], F32R, late)
        late.close()

        S = ctx.enter_context(nc.psum_tensor("S", [P, 4, BANK], F32))
        TP = ctx.enter_context(nc.psum_tensor("TP", [P, TB, BANK], F32))
        O = ctx.enter_context(nc.psum_tensor("O", [P, BANK], F32))

        mask_in, x_in, wq_in, bias_in = sem("mask_in"), sem("x_in"), sem("wq_in"), sem("bias_in")
        consts = sem("consts")
        ones_made = sem("ones_made")
        mask_made, mask_stored = sem("mask_made"), sem("mask_stored")
        ln_stat, ln_mv, ln_std, ln_rstd, ln_done = (sem(n) for n in ("ln_stat", "ln_mv", "ln_std", "ln_rstd", "ln_done"))
        xT_mm, xT_out = sem("xT_mm"), sem("xT_out")
        q_mm, q_made, q_hi_out, q_lo_out, q_stored = sem("q_mm"), sem("q_made"), sem("q_hi_out"), sem("q_lo_out"), sem("q_stored")
        wraw_in = [sem("wraw_in_k"), sem("wraw_in_v")]
        craw_in = [sem("craw_in_0"), sem("craw_in_1")]
        w_hi_made, w_made = sem("w_hi_made"), sem("w_made")
        c_hi_made, c01_made, c_made = sem("c_hi_made"), sem("c01_made"), sem("c_made")
        k_mm, k_hi_out, k_out = sem("k_mm"), sem("k_hi_out"), sem("k_out")
        k_stacked = [[sem(f"k_stacked_{g}_{n}") for n in range(2)] for g in range(HPC)]
        v_mm, v_hi_out, v_out = sem("v_mm"), sem("v_hi_out"), sem("v_out")
        q_stacked = sem("q_stacked")
        s_mm, nmx_made, exp_done = sem("s_mm"), sem("nmx_made"), sem("exp_done")
        t_mm, pt_hi_out, pt_out, pv_mm, o_out = sem("t_mm"), sem("pt_hi_out"), sem("pt_out"), sem("pv_mm"), sem("o_out")
        fac_step, fac_exp, fac_made, rb_mm = sem("fac_step"), sem("fac_exp"), sem("fac_made"), sem("rb_mm")
        o_normed, o_summed, fold_made, fold_mm, a_done = (
            sem(n) for n in ("o_normed", "o_summed", "fold_made", "fold_mm", "a_done"))
        late_w = [sem(f"late_w{i}") for i in range(5)]
        x1_in, row_in, rb_v_in, ffn_small_in = sem("x1_in"), sem("row_in"), sem("rb_v_in"), sem("ffn_small_in")
        bo_added, oproj_mm, x1_done = sem("bo_added"), sem("oproj_mm"), sem("x1_done")
        sp_mm = sem("sp_mm")
        sq_out, sk_out, sv_out, causal_made = sem("sq_out"), sem("sk_out"), sem("sv_out"), sem("causal_made")
        ss_mm, ss_max, ss_exp, ss_rd, ss_normed, sT_mm, sT_out = (
            sem(n) for n in ("ss_mm", "ss_max", "ss_exp", "ss_rd", "ss_normed", "sT_mm", "sT_out"))
        so_mm, so_out, bo2_added, oproj2_mm, x2_done = (sem(n) for n in ("so_mm", "so_out", "bo2_added", "oproj2_mm", "x2_done"))
        x3_hi_made, x3_made = sem("x3_hi_made"), sem("x3_made")
        gate_mm, gate_step, gate_exp, combT_mm, combT_out, b2_mm, acc_step = (
            sem(n) for n in ("gate_mm", "gate_step", "gate_exp", "combT_mm", "combT_out", "b2_mm", "acc_step"))
        eraw_in = [sem(f"eraw_in_{n}") for n in ("w1", "w3", "w2")]
        e_hi_made, e_made = sem("e_hi_made"), sem("e_made")
        h_mm, silu_made, g_made, g_hi_made, g_split, y_mm = (
            sem(n) for n in ("h_mm", "silu_made", "g_made", "g_hi_made", "g_split", "y_mm"))
        out_stored = sem("out_stored")

        KST = 3 * 16
        QST = 2 * 16
        QSTORED = 3 * HPC * 16
        PROJ = [x for c in range(NCH - 2) for x in (("K", c), ("V", c))] + [
            ("K", NCH - 2), ("K", NCH - 1), ("V", NCH - 2), ("V", NCH - 1)]
        PROJ.insert(PROJ.index(("V", NCH // 2 + 1)) + 1, ("S", 0))
        PROJ.insert(PROJ.index(("K", NCH - 2)) + 1, ("S", 1))
        PROJ.insert(PROJ.index(("V", 0)) + 1, ("fold", 0))

        def unit(u):
            return 2 * (u // 4) + u % 2, u % 4 // 2

        def f32(ap):
            return ap.bitcast(F32)

        def all_stages(eng, first, stage):
            first()
            stage(0, False)
            with eng.Fori(1, STAGES - 1) as s:
                stage(s, False)
            stage(STAGES - 1, True)

        def all_experts(eng, expert):
            expert(0, 0, True, False)
            expert(1, 1, False, False)
            with eng.Fori(1, NE // 2) as k:
                expert(2 * k, 0, False, False)
                expert(2 * k + 1, 1, False, False)
            expert(NE - 1, 0, False, True)

        def e_hi(slot):
            return (e_hi0, e_hi1)[slot]

        def e_lo(slot):
            return (e_lo0, e_lo1)[slot]

        def wait_chunk(eng, s, c):
            if c < 2:
                eng.wait_ge(c01_made, 2 * s + c + 1)
            else:
                eng.wait_ge(c_made, (NCH - 2) * s + c - 1)

        def oproj_bank(b):
            return 3 if b == 0 else 1

        def up_bank(f):
            return TP[:, f, :] if f < 3 else O[:, :]

        block = ctx.enter_context(nc.Block())

        @block.sync
        def _(sp):
            def first():
                sp.dma_start(x_a, x.rearrange("b t d -> t b d")).then_inc(x_in, 16)
                sp.dma_start(wq_a, xwT[0]).then_inc(wq_in, 16)
                sp.dma_start(bias_x[:, :, :], xbias).then_inc(bias_in, 16)
                sp.dma_start(bias_a[:, :, :], abias).then_inc(bias_in, 16)
                sp.dma_start(mask_u, mask).then_inc(mask_in, 16)
                sp.wait_ge(mask_made, 5)
                sp.dma_start(mask_dram, f32(mask_r)).then_inc(mask_stored, 16)
                sp.wait_ge(q_lo_out, 2)
                for g in range(HPC):
                    for n, part in enumerate((q_hi, q_hi, q_lo)):
                        sp.dma_start(q_dram[n * HD:(n + 1) * HD, :, g, :],
                                     f32(part[g * HD:(g + 1) * HD])).then_inc(q_stored, 16)
                sp.wait_ge(mask_stored, 16)
                sp.wait_ge(q_stored, QSTORED)

            def stage(s, last):
                b, half = s // 2, s % 2
                for c in range(NCH):
                    if c == 0:
                        sp.wait_ge(s_mm, UNITS * s)
                        sp.dma_start(f32(qst[0:3 * HD, :, :, :]).rearrange("p o g t -> p (o g) t"),
                                     q_dram[:, bass.ds(half * OC, OC), :, bass.ds(b * T, T)].rearrange(
                                         "p o g t -> p (o g) t")).then_inc(q_stacked, 16)
                        sp.dma_start(f32(kst[3 * HD:KROWS, :, :, :]).rearrange("p o g k -> p (o g) k"),
                                     mask_dram[bass.ds(b, 1), :].unsqueeze(1).to_broadcast([1, HS, S2])
                                     ).then_inc(q_stacked, 16)
                    if c % 2:
                        sp.wait_ge(k_hi_out, s * NCH + c + 1)
                        for g in range(HPC):
                            rows = slice(g * HD, (g + 1) * HD)
                            for at, part in ((0, 0), (2 * HD, 0), (HD, 1)):
                                if g == 0 and part == 1:
                                    sp.wait_ge(k_out, s * NCH + c + 1)
                                sp.dma_start(f32(kst[at:at + HD, :, g, (c - 1) * CK:(c + 1) * CK]),
                                             k_parts[c // 2 % 2][rows, part]).then_inc(k_stacked[g][c // 2 % 2], 16)

            all_stages(sp, first, stage)

            sp.wait_ge(v_mm, STAGES * NCH)
            sp.dma_start(wo_x[:, :, :], xwT[3]).then_inc(late_w[0], 16)
            sp.dma_start(x1[:, :, :], x.rearrange("b t d -> t b d")).then_inc(x1_in, 16)
            sp.dma_start(rb_x[:, :], rowbias[0].partition_broadcast(P)).then_inc(row_in, 16)
            sp.dma_start(rb_a[:, :], rowbias[1].partition_broadcast(P)).then_inc(row_in, 16)
            sp.dma_start(swq[:, :, :], awT[0]).then_inc(late_w[1], 16)
            sp.wait_ge(a_done, STAGES * OC)
            for n, (w, src) in enumerate(((swk, awT[1]), (swv, awT[2]), (swo, awT[3]))):
                sp.dma_start(w[:, :, :], src).then_inc(late_w[2 + n], 16)
            sp.dma_start(rb_v[:, :], rowbias[2].partition_broadcast(P)).then_inc(rb_v_in, 16)

            def ffn_small():
                sp.dma_start(gw[:, :, :], gateT).then_inc(ffn_small_in, 16)
                sp.dma_start(ebs[:, :, :, :], eb).then_inc(ffn_small_in, 16)
                sp.dma_start(b2s[:, :], eb2).then_inc(ffn_small_in, 16)

            def expert(e, slot, first_one, last_one):
                for k, w in enumerate((w1, w3, w2)):
                    if not first_one:
                        sp.wait_ge(e_made, 3 * e + k - 2)
                    sp.dma_start(eraw[:, k], w[e] if isinstance(e, int) else w[bass.ds(e, 1)].rearrange(
                        "e p c d -> (e p) c d")).then_inc(eraw_in[k], 16)
                if first_one:
                    ffn_small()

            all_experts(sp, expert)
            for b in range(B):
                sp.wait_ge(acc_step, B * NE + b + 1)
                sp.dma_start(out[b], x1[:, b, :]).then_inc(out_stored, 16)
            sp.wait_ge(out_stored, 16 * B)

        @block.gpsimd
        def _(pool):
            def first():
                constants()
                folding()

            def stage(s, last):
                if last:
                    return
                for n in range(2):
                    pool.wait_ge(w_hi_made, 2 * s + 3 + n)
                    nc.gpsimd.tensor_tensor(w_lo[:, n], wraw[:, n], f32(w_hi[:, n]), ALU.subtract).then_inc(w_made, 1)
                for c in range(2):
                    pool.wait_ge(c_hi_made, (s + 1) * NCH + c + 1)
                    nc.gpsimd.tensor_tensor(c_lo[:, c], craw[:, c], f32(c_hi[:, c]), ALU.subtract).then_inc(c01_made, 1)

            def constants():
                nc.gpsimd.memset(ident[:, :], 0.0).then_inc(consts, 1)
                nc.gpsimd.memset(epsc[:, :], EPS).then_inc(consts, 1)
                pool.wait_ge(consts, 2)
                nc.gpsimd.affine_select(out=ident[:, :], in_=ident[:, :], compare_op=ALU.not_equal, fill=1.0,
                                        base=0, pattern=[[-1, P]], channel_multiplier=1).then_inc(consts, 1)

            def folding():
                nc.gpsimd.memset(fold[:, :, :], 0.0).then_inc(fold_made, 1)
                pool.wait_ge(fold_made, 1)
                pool.wait_ge(consts, 3)
                for q in range(HPC):
                    rows = slice(q * HD, (q + 1) * HD)
                    for n in range(2):
                        at = n * 2 * HD + q // 2 * HD
                        nc.gpsimd.tensor_copy(fold[rows, n, at:at + HD], ident[rows, rows]).then_inc(fold_made, 1)
                pool.wait_ge(fold_made, 1 + 2 * HPC)

            all_stages(pool, first, stage)
            pool.wait_ge(a_done, STAGES * OC)
            nc.gpsimd.memset(causal[:, :], 0.0).then_inc(consts, 1)
            pool.wait_ge(consts, 4)
            nc.gpsimd.affine_select(out=causal[:, :], in_=causal[:, :], compare_op=ALU.is_ge, fill=NEG,
                                    base=0, pattern=[[-1, T]], channel_multiplier=1).then_inc(consts, 1)
            for n in range(B * HPC):
                pool.wait_ge(ss_rd, n + 1)
                nc.gpsimd.tensor_tensor(sc_s[:, n], sc_s[:, n], srd[:, n, :].unsqueeze(2).to_broadcast([P, IC, T]),
                                        ALU.mult).then_inc(ss_normed, 1)

        @block.tensor
        def _(pe):
            def products(out_ap, a, b, ready=lambda ic: None):
                for ic in range(IC):
                    ready(ic)
                    (ah, al), (bh, bl) = a(ic), b(ic)
                    for n, (l, r) in enumerate(((ah, bh), (ah, bl), (al, bh))):
                        mm = nc.tensor.matmul(out_ap, l, r, start=(ic == 0 and n == 0),
                                              stop=(ic == IC - 1 and n == 2))
                return mm

            def plain(out_ap, a, b):
                for ic in range(IC):
                    mm = nc.tensor.matmul(out_ap, a(ic), b(ic), start=(ic == 0), stop=(ic == IC - 1))
                return mm

            def transpose_x(n, src):
                for b in range(B):
                    pe.wait_ge(ln_done, B * n + b + 1)
                    for ic in range(IC):
                        mm = nc.tensor.transpose(TP[:, b, ic * P:(ic + 1) * P], src[:, b, ic * P:(ic + 1) * P],
                                                 ident[:, :])
                    mm.then_inc(xT_mm, 1)

            def first():
                pe.wait_ge(consts, 3)
                pe.wait_ge(ones_made, 1)
                transpose_x(0, xn_a)
                pe.wait_ge(wq_in, 16)
                pe.wait_ge(xT_out, B)
                for oc in range(IC):
                    mm = plain(S[:, oc // 2, (oc % 2) * TOK:(oc % 2 + 1) * TOK],
                               lambda ic: wq_a[:, ic, oc * P:(oc + 1) * P], lambda ic: xnT_a[:, ic, :])
                    if oc % 2:
                        mm.then_inc(q_mm, 1)

            def project_k(s, c):
                if c == 0:
                    pe.wait_ge(w_made, 2 * s + 2)
                wait_chunk(pe, s, c)
                if c >= 2:
                    pe.wait_ge(k_out, s * NCH + c - 1)
                for o in range(OC):
                    cols = slice(o * P, (o + 1) * P)
                    mm = products(TP[:, c % 2, o * CK:(o + 1) * CK],
                                  lambda ic: (w_hi[:, 0, ic, cols], w_lo[:, 0, ic, cols]),
                                  lambda ic: (c_hi[:, c % 2, ic, :], c_lo[:, c % 2, ic, :]))
                mm.then_inc(k_mm, 1)

            def project_v(s, c):
                bank = TP[:, 2, :] if c % 2 == 0 else O[:, :]
                if c >= 2:
                    pe.wait_ge(v_out, s * NCH + c - 1)
                if c == 1:
                    pe.wait_ge(o_out, s * PAIRS)
                for k in range(CK // P):
                    keys = slice(k * P, (k + 1) * P)
                    mm = products(bank[:, k * HW:(k + 1) * HW],
                                  lambda ic: (c_hi[:, c % 2, ic, keys], c_lo[:, c % 2, ic, keys]),
                                  lambda ic: (w_hi[:, 1, ic, :], w_lo[:, 1, ic, :]))
                mm.then_inc(v_mm, 1)

            def scores(s, u):
                h, half = unit(u)
                if u == 0:
                    pe.wait_ge(q_stacked, QST * (s + 1))
                    pe.wait_ge(o_normed, s)
                half_in, all_in = KST * (NCH // 4 * s + 1), KST * (NCH // 4) * (s + 1)
                for g, n, count in {0: [(0, 0, half_in), (0, 1, half_in)], 1: [(1, 0, half_in), (1, 1, half_in)],
                                    2: [(0, 0, all_in), (0, 1, all_in)], 3: [(1, 0, all_in), (1, 1, all_in)],
                                    4: [(2, 0, all_in), (3, 0, all_in), (2, 1, half_in)],
                                    5: [(2, 1, all_in), (3, 1, all_in)]}.get(u, []):
                    pe.wait_ge(k_stacked[g][n], count)
                if u == 1:
                    pe.wait_ge(a_done, OC * s)
                if u >= 2:
                    pe.wait_ge(exp_done, UNITS * s + u - 1)
                for n in range(2):
                    keys = slice((2 * half + n) * BANK, (2 * half + n + 1) * BANK)
                    mm = nc.tensor.matmul(S[:, 2 * (u % 2) + n, :], qst[0:KROWS, h // HPC, h % HPC, :],
                                          kst[0:KROWS, h // HPC, h % HPC, keys], start=True, stop=True)
                mm.then_inc(s_mm, 1)

            def fold_outputs(s):
                if isinstance(s, int) and s == 0:
                    return
                pe.wait_ge(fold_made, 1 + 2 * HPC)
                pe.wait_ge(o_summed, s)
                for n in range(2):
                    mm = nc.tensor.matmul(S[:, 2, 0:OC * T].rearrange("p (o t) -> p o t", o=OC), fold[:, n, :],
                                          oraw[:, :, 0, :].rearrange("p (o n) t -> p n o t", n=2)[:, n],
                                          start=(n == 0), stop=(n == 1))
                mm.then_inc(fold_mm, 1)

            def transposes(s, g):
                p, j = g // STEPS, g % STEPS
                if j % (STEPS // 2) == 0:
                    pe.wait_ge(exp_done, UNITS * s + 4 * p + 4 * j // STEPS + 2)
                if g >= TB:
                    pe.wait_ge(pt_out, s * STAGE_STEPS + g - TB + 1)
                elif g == 0:
                    pe.wait_ge(k_out, (s + 1) * NCH)
                elif g == 2:
                    pe.wait_ge(v_out, s * NCH + NCH - 1)
                for k in range(2):
                    for hl in range(2):
                        kt = 2 * j + k
                        mm = nc.tensor.transpose(TP[:, g % TB, (2 * k + hl) * P:(2 * k + hl + 1) * P],
                                                 prob[:, (2 * p + hl) % 4, kt * P:(kt + 1) * P], ident[:, :])
                mm.then_inc(t_mm, 1)

            def times_v(s, g):
                p, j = g // STEPS, g % STEPS
                pe.wait_ge(pt_out, s * STAGE_STEPS + g + 1)
                if g == 0:
                    pe.wait_ge(v_out, (s + 1) * NCH)
                elif j == 0:
                    pe.wait_ge(o_out, s * PAIRS + p)
                half = j // (STEPS // 2)
                for k in range(2):
                    kt, pc = 2 * j + k, slice(k * 2 * P, (k + 1) * 2 * P)
                    for n, pt in enumerate((pt_hi, pt_lo)):
                        mm = nc.tensor.matmul(O[:, half * 2 * P:(half + 1) * 2 * P],
                                              v_pk[:, kt, 2 * p:2 * p + 2, :, :].rearrange("p h n d -> p (h n d)"),
                                              pt[:, g % PB, pc], start=(kt % (KT // 2) == 0 and n == 0),
                                              stop=(kt % (KT // 2) == KT // 2 - 1 and n == 1))
                mm.then_inc(pv_mm, 1)

            def stage(s, last):
                for what, n in PROJ:
                    if what == "fold":
                        fold_outputs(s)
                    else:
                        {"K": project_k, "V": project_v, "S": scores}[what](s, n)
                for g in range(STAGE_STEPS + LAG):
                    if g < STAGE_STEPS:
                        if g % STEPS == LAG - 1 and g >= LAG:
                            times_v(s, g - LAG)
                        transposes(s, g)
                        if g in SCORES_AT:
                            scores(s, SCORES_AT[g])
                    if g == STAGE_STEPS:
                        pe.wait_ge(fac_made, s + 1)
                        for p in range(PAIRS):
                            for i in range(2):
                                mm = nc.tensor.matmul(S[:, p // 2, (2 * (p % 2) + i) * T:(2 * (p % 2) + i + 1) * T],
                                                      fac_rep[:, p, i, :, :].rearrange("p l d -> p (l d)"),
                                                      ident[:, :], start=True, stop=True)
                        mm.then_inc(rb_mm, 1)
                    if g >= LAG and (g >= STAGE_STEPS or g % STEPS != LAG - 1):
                        times_v(s, g - LAG)

            all_stages(pe, first, stage)

            for b in range(B):
                if b == 0:
                    pe.wait_ge(late_w[0], 16)
                    pe.wait_ge(a_done, STAGES // B * OC)
                else:
                    fold_outputs(STAGES)
                    pe.wait_ge(a_done, STAGES * OC)
                plain(S[:, oproj_bank(b), :], lambda ic: aT[:, ic, b * T:(b + 1) * T], lambda ic: wo_x[:, ic, :]).then_inc(oproj_mm, 1)
            transpose_x(1, xn)
            pe.wait_ge(xT_out, 2 * B)
            pe.wait_ge(x1_done, B)
            for n, w in enumerate((swq, swk)):
                pe.wait_ge(late_w[1 + n], 16)
                for oc in range(IC):
                    mm = plain(S[:, 2 * n + oc // 2, (oc % 2) * TOK:(oc % 2 + 1) * TOK],
                               lambda ic: w[:, ic, oc * P:(oc + 1) * P], lambda ic: xnT[:, ic, :])
                    if oc % 2:
                        mm.then_inc(sp_mm, 1)

            def self_v(b):
                pe.wait_ge(late_w[3], 16)
                plain(TP[:, b, :], lambda ic: xnT[:, ic, b * T:(b + 1) * T], lambda ic: swv[:, ic, :]).then_inc(sp_mm, 1)

            def self_scores(n):
                b, g = n // HPC, n % HPC
                if n == 0:
                    pe.wait_ge(sq_out, 2)
                    pe.wait_ge(sk_out, 2)
                    pe.wait_ge(causal_made, 2)
                elif n >= HPC:
                    pe.wait_ge(ss_exp, n - HPC + 1)
                nc.tensor.matmul(S[:, g, :], ident_r[:, :], causal_r[:, :].unsqueeze(1).to_broadcast([P, IC, T]),
                                 start=True, stop=False)
                for oc in range(IC):
                    mm = nc.tensor.matmul(S[:, g, oc * T:(oc + 1) * T],
                                          q_s[g * HD:(g + 1) * HD, oc, b * T:(b + 1) * T],
                                          k_s[g * HD:(g + 1) * HD, oc, b * T:(b + 1) * T],
                                          start=False, stop=(oc == IC - 1))
                mm.then_inc(ss_mm, 1)

            def self_transposes(n):
                pe.wait_ge(ss_normed, n + 1)
                if n < 2:
                    pe.wait_ge(sv_out, n + 1)
                else:
                    pe.wait_ge(sT_out, n - 1)
                for oc in range(IC):
                    mm = nc.tensor.transpose(TP[:, n % 2, oc * T:(oc + 1) * T], sc_s[:, n, oc, :], ident[:, :])
                mm.then_inc(sT_mm, 1)

            def self_times_v(n):
                b, g = n // HPC, n % HPC
                pe.wait_ge(sT_out, n + 1)
                out_bank = TP[:, 2, :] if b == 0 else O[:, :]
                for oc in range(IC):
                    h = HPC * oc + g
                    mm = nc.tensor.matmul(out_bank[g * HD:(g + 1) * HD, oc * T:(oc + 1) * T],
                                          v_s[:, b, h * HD:(h + 1) * HD], pt_s[:, n % PTS, oc, :], start=True, stop=True)
                mm.then_inc(so_mm, 1)

            def self_oproj(b):
                pe.wait_ge(late_w[4], 16)
                pe.wait_ge(so_out, b + 1)
                pe.wait_ge(ss_exp, HPC + b + 1)
                plain(S[:, b, :], lambda ic: a2T[:, ic, b * T:(b + 1) * T], lambda ic: swo[:, ic, :]).then_inc(oproj2_mm, 1)

            self_v(0)
            for n in range(HPC):
                self_scores(n)
            self_v(1)
            for n in range(B * HPC):
                self_transposes(n)
                if n + HPC < B * HPC:
                    self_scores(n + HPC)
                if n == B * HPC - 1:
                    self_oproj(0)
                if n > 0:
                    self_times_v(n - 1)
            self_times_v(B * HPC - 1)
            self_oproj(1)
            transpose_x(2, xn)

            def gate():
                pe.wait_ge(ffn_small_in, 48)
                pe.wait_ge(xT_out, 3 * B)
                for b in range(B):
                    mm = plain(TP[:, 2, b * E:(b + 1) * E], lambda ic: xnT[:, ic, b * T:(b + 1) * T], lambda ic: gw[:, ic, :])
                mm.then_inc(gate_mm, 1)

            def weights_transposed():
                pe.wait_ge(gate_step, GATE_STEPS)
                for b in range(B):
                    mm = nc.tensor.transpose(S[0:NE, 0, b * T:(b + 1) * T], comb[:, b, :], ident[:, :])
                mm.then_inc(combT_mm, 1)

            def second_biases():
                pe.wait_ge(combT_out, 1)
                for b in range(B):
                    mm = nc.tensor.matmul(S[:, B + b, :], combT[:, b * T:(b + 1) * T], b2s[:, :], start=True, stop=True)
                mm.then_inc(b2_mm, 1)

            def up(e, slot, f):
                if f == 0:
                    pe.wait_ge(e_made, 3 * e + 2)
                if not isinstance(e, int) or e > 0:
                    pe.wait_ge(g_made, FC * (e - 1) + f + 1)
                else:
                    if f == 0:
                        pe.wait_ge(x3_made, B)
                    if f < B:
                        pe.wait_ge(xT_out, 2 * B + f + 1)
                    if f == 2:
                        pe.wait_ge(gate_exp, B)
                for n in range(2):
                    cols = slice(f * P, (f + 1) * P)
                    mm = products(up_bank(f)[:, n * TOK:(n + 1) * TOK],
                                  lambda ic: (e_hi(slot)[:, n, ic, cols], e_lo(slot)[:, n, ic, cols]),
                                  lambda ic: (x3_hi[:, ic, :], x3_lo[:, ic, :]))
                mm.then_inc(h_mm, 1)

            def down(e, slot):
                pe.wait_ge(e_made, 3 * e + 3)
                pe.wait_ge(acc_step, B * e)

                def inner_ready(ic):
                    pe.wait_ge(g_split, FC * e + ic + 1)

                for b in range(B):
                    mm = products(S[:, 2 * slot + b, :],
                                  lambda ic: (g_hi[:, slot, ic, b * T:(b + 1) * T], g_lo[:, slot, ic, b * T:(b + 1) * T]),
                                  lambda ic: (e_hi(slot)[:, 2, ic, :], e_lo(slot)[:, 2, ic, :]),
                                  *([inner_ready] if b == 0 else []))
                    mm.then_inc(y_mm, 1)

            def expert(e, slot, first_one, last_one):
                for f in range(FC):
                    if f == 2 and isinstance(e, int) and e == 1:
                        second_biases()
                    if f == 2 and not first_one:
                        down(e - 1, 1 - slot)
                    up(e, slot, f)
                    if f == 0 and first_one:
                        gate()
                    if f == 2 and first_one:
                        weights_transposed()
                if last_one:
                    down(e, slot)

            all_experts(pe, expert)

        @block.scalar
        def _(act):
            def load_w(s):
                act.wait_ge(w_made, 2 * s)
                for n in range(2):
                    act.dma_start(wraw[:, n], xwT[1 + n][:, :, bass.ds((s % 2) * HW, HW)]).then_inc(wraw_in[n], 16)

            def load_c(s, c):
                act.dma_start(craw[:, c % 2], ctxT[s // 2, c]).then_inc(craw_in[c % 2], 16)

            def ln_sqrt(n, b):
                act.wait_ge(ln_mv, B * n + b + 1)
                nc.scalar.activation(std[:, b:b + 1], mv[:, b, 1:2], ACT.Sqrt, bias=epsc[:, 0:1]).then_inc(ln_std, 1)

            def split_w(s, n):
                act.wait_ge(wraw_in[n], 16 * s + 16)
                nc.scalar.copy(w_hi[:, n], wraw[:, n]).then_inc(w_hi_made, 1)

            def split_c(s, c):
                act.wait_ge(craw_in[c % 2], 16 * (s * (NCH // 2) + c // 2 + 1))
                nc.scalar.copy(c_hi[:, c % 2], craw[:, c % 2]).then_inc(c_hi_made, 1)

            def first():
                load_w(0)
                load_c(0, 0)
                load_c(0, 1)
                act.wait_ge(consts, 2)
                for b in range(B):
                    ln_sqrt(0, b)
                split_w(0, 0)
                split_w(0, 1)
                split_c(0, 0)
                split_c(0, 1)
                for n in range(2):
                    act.wait_ge(q_made, n + 1)
                    nc.scalar.copy(q_hi[:, 2 * n:2 * n + 2, :], q_raw[:, 2 * n:2 * n + 2, :]).then_inc(q_hi_out, 1)
                act.wait_ge(mask_stored, 16)

            def outputs_out(s, p):
                act.wait_ge(pv_mm, s * STAGE_STEPS + (p + 1) * STEPS)
                for hl in range(2):
                    rows = slice(hl * 2 * HD, (hl + 1) * 2 * HD)
                    i = nc.scalar.copy(oraw[rows, p, :, :],
                                       O[rows, :].rearrange("p (i l t) -> p i l t", i=2, l=2)[:, :, hl, :])
                i.then_inc(o_out, 1)

            def exps(s, u):
                h, half = unit(u)
                act.wait_ge(nmx_made, s * UNITS + u + 1)
                if u == 0:
                    act.wait_ge(t_mm, s * STAGE_STEPS)
                elif u >= 8:
                    act.wait_ge(t_mm, s * STAGE_STEPS + (u // 4 - 1) * STEPS)
                at = slice(half * 2 * BANK, (half + 1) * 2 * BANK)
                one = (slice(None), h // HPC, half, slice(h % HPC, h % HPC + 1))
                nc.scalar.activation(prob[:, h % 4, at], S[:, 2 * (u % 2):2 * (u % 2) + 2, :].rearrange("p n k -> p (n k)"),
                                     ACT.Exp, bias=nmx[one], accum_out=den[one]).then_inc(exp_done, 1)

            def stage(s, last):
                for what, n in PROJ:
                    if what == "K":
                        if n + 2 < NCH or not last:
                            wait_chunk(act, s, n)
                            load_c(s + (n + 2) // NCH, (n + 2) % NCH)
                        if n == 1 and not last:
                            load_w(s + 1)
                    elif what == "V":
                        act.wait_ge(v_mm, s * NCH + n + 1)
                        src = TP[:, 2, :] if n % 2 == 0 else O[:, :]
                        nc.scalar.copy(v_pk[:, 2 * n:2 * n + 2, :, 0, :],
                                       src.rearrange("p (k h d) -> p k h d", k=2, h=HS)).then_inc(v_hi_out, 1)
                        if n + 2 < NCH:
                            split_c(s, n + 2)
                    elif what == "S":
                        exps(s, n)
                for g in range(STAGE_STEPS):
                    p, j = g // STEPS, g % STEPS
                    if j == LAG - 1 and p > 0:
                        outputs_out(s, p - 1)
                    act.wait_ge(t_mm, s * STAGE_STEPS + g + 1)
                    if g >= PB:
                        act.wait_ge(pv_mm, s * STAGE_STEPS + g - PB + 1)
                    nc.scalar.copy(pt_hi[:, g % PB, :], TP[:, g % TB, :]).then_inc(pt_hi_out, 1)
                    if g in EXP_AT:
                        exps(s, EXP_AT[g])
                    if g == FAC_AT + 1:
                        act.wait_ge(fac_step, 5 * s + 2)
                        nc.scalar.activation(fac[:, :, :, :], fac[:, :, :, :], ACT.Exp).then_inc(fac_exp, 1)
                    if not last:
                        if g in SPLIT_W_AT:
                            split_w(s + 1, SPLIT_W_AT[g])
                        if g in SPLIT_C_AT:
                            split_c(s + 1, SPLIT_C_AT[g])

                outputs_out(s, PAIRS - 1)

            all_stages(act, first, stage)

            for b in range(B):
                ln_sqrt(1, b)

            def split_e(e, slot, k):
                act.wait_ge(eraw_in[k], 16 * e + 16)
                if not isinstance(e, int) or e >= 2:
                    if k < 2:
                        act.wait_ge(h_mm, FC * (e - 1))
                    else:
                        act.wait_ge(y_mm, B * (e - 1))
                nc.scalar.copy(e_hi(slot)[:, k], eraw[:, k]).then_inc(e_hi_made, 1)

            act.wait_ge(consts, 5)
            nc.scalar.copy(causal_r[:, :], causal[:, :]).then_inc(causal_made, 1)
            nc.scalar.copy(ident_r[:, :], ident[:, :]).then_inc(causal_made, 1)
            for k in range(2):
                split_e(0, 0, k)
            for n in range(2):
                act.wait_ge(sp_mm, 3 + n)
                for o in range(2):
                    oc = 2 * n + o
                    i = nc.scalar.activation(k_s[:, oc, :], S[:, 2 + n, o * TOK:(o + 1) * TOK], ACT.Identity,
                                             bias=bias_a[:, 1, oc:oc + 1])
                i.then_inc(sk_out, 1)
            split_e(0, 0, 2)
            for n in range(B * HPC):
                act.wait_ge(ss_max, n + 1)
                for oc in range(IC):
                    i = nc.scalar.activation(sc_s[:, n, oc, :], S[:, n % HPC, oc * T:(oc + 1) * T], ACT.Exp,
                                             bias=snmx[:, n, oc:oc + 1], accum_out=ssum[:, n, oc:oc + 1])
                i.then_inc(ss_exp, 1)
            for b in range(B):
                ln_sqrt(2, b)
            for b in range(B):
                act.wait_ge(xT_mm, 2 * B + b + 1)
                nc.scalar.copy(x3_hi[:, :, b * T:(b + 1) * T], TP[:, b, :].rearrange("p (c t) -> p c t", c=IC)).then_inc(x3_hi_made, 1)
            act.wait_ge(oproj2_mm, B)
            for k in range(2):
                split_e(1, 1, k)
            act.wait_ge(gate_step, 1)
            for b in range(B):
                nc.scalar.activation(sc16[:, b, 0:E], TP[:, 2, b * E:(b + 1) * E], ACT.Exp,
                                     bias=gsm[:, b, 0:1], accum_out=gsm[:, b, 1:2]).then_inc(gate_exp, 1)

            def expert(e, slot, first_one, last_one):
                for f in range(FC):
                    if f < 3 and not last_one and not (first_one and f < 2):
                        split_e(e + 1, 1 - slot, f)
                    act.wait_ge(h_mm, FC * e + f + 1)
                    act.wait_ge(ffn_small_in, 48)
                    nc.scalar.activation(silu[:, f % 2, :], up_bank(f)[:, 0:TOK], ACT.Silu,
                                         bias=ebs[:, 0, bass.ds(e, 1), f]).then_inc(silu_made, 1)
                    act.wait_ge(g_made, FC * e + f + 1)
                    if f == 0 and (not isinstance(e, int) or e >= 2):
                        act.wait_ge(y_mm, B * (e - 1))
                    nc.scalar.copy(g_hi[:, slot, f, :], gf[:, f % 2, :]).then_inc(g_hi_made, 1)

            all_experts(act, expert)

        @block.vector
        def _(dve):
            def layer_norm(n, b, src, dst):
                nc.vector.bn_stats(stat[:, b, :], src[:, b, :]).then_inc(ln_stat, 1)
                dve.wait_ge(ln_stat, B * n + b + 1)
                nc.vector.bn_aggr(mv[:, b, :], stat[:, b, :]).then_inc(ln_mv, 1)
                dve.wait_ge(ln_std, B * n + b + 1)
                nc.vector.reciprocal(rstd[:, b:b + 1], std[:, b:b + 1]).then_inc(ln_rstd, 1)
                dve.wait_ge(ln_rstd, B * n + b + 1)
                nc.vector.tensor_scalar(dst[:, b, :], src[:, b, :], mv[:, b, 0:1], rstd[:, b:b + 1],
                                        ALU.subtract, ALU.mult).then_inc(ln_done, 1)

            def transposed_out(n, b, dst):
                dve.wait_ge(xT_mm, B * n + b + 1)
                nc.vector.tensor_copy(dst[:, :, b * T:(b + 1) * T],
                                      TP[:, b, :].rearrange("p (c t) -> p c t", c=IC)).then_inc(xT_out, 1)

            def split_w(s, n):
                dve.wait_ge(w_hi_made, 2 * s + n + 1)
                nc.vector.tensor_tensor(w_lo[:, n], wraw[:, n], f32(w_hi[:, n]), ALU.subtract).then_inc(w_made, 1)

            def split_c(s, c):
                dve.wait_ge(c_hi_made, s * NCH + c + 1)
                nc.vector.tensor_tensor(c_lo[:, c % 2], craw[:, c % 2], f32(c_hi[:, c % 2]), ALU.subtract).then_inc(c01_made if c < 2 else c_made, 1)

            def first():
                nc.vector.memset(f32(qst[3 * HD:KROWS, :, :, :]), 1.0).then_inc(ones_made, 1)
                dve.wait_ge(x_in, 16)
                for b in range(B):
                    layer_norm(0, b, x_a, xn_a)
                for b in range(B):
                    transposed_out(0, b, xnT_a)
                split_w(0, 0)
                split_w(0, 1)
                split_c(0, 0)
                split_c(0, 1)
                dve.wait_ge(mask_in, 16)
                nc.vector.tensor_reduce(mask_nan[:, 0:1], mask_u, AX.X, ALU.min).then_inc(mask_made, 1)
                dve.wait_ge(mask_made, 1)
                nc.vector.tensor_scalar(mask_nan[:, 0:1], mask_nan[:, 0:1], -3.0e38, 10.0, ALU.mult, ALU.mult).then_inc(mask_made, 1)
                dve.wait_ge(mask_made, 2)
                nc.vector.tensor_tensor(mask_nan[:, 1:2], mask_nan[:, 0:1], mask_nan[:, 0:1], ALU.subtract).then_inc(mask_made, 1)
                dve.wait_ge(mask_made, 3)
                nc.vector.tensor_scalar(mask_r, mask_u, NEG, mask_nan[:, 1:2], ALU.mult, ALU.add).then_inc(mask_made, 2)
                dve.wait_ge(bias_in, 32)
                for n in range(2):
                    dve.wait_ge(q_mm, n + 1)
                    for o in range(2):
                        oc = 2 * n + o
                        i = nc.vector.tensor_scalar(q_raw[:, oc, :], S[:, n, o * TOK:(o + 1) * TOK],
                                                    bias_x[:, 0, oc:oc + 1], SC, ALU.add, ALU.mult)
                    i.then_inc(q_made, 1)
                for n in range(2):
                    dve.wait_ge(q_hi_out, n + 1)
                    nc.vector.tensor_tensor(q_lo[:, 2 * n:2 * n + 2, :], q_raw[:, 2 * n:2 * n + 2, :],
                                            f32(q_hi[:, 2 * n:2 * n + 2, :]), ALU.subtract).then_inc(q_lo_out, 1)
                dve.wait_ge(mask_stored, 16)

            def maximum(s, u):
                h, half = unit(u)
                if u == 0:
                    dve.wait_ge(exp_done, UNITS * s)
                dve.wait_ge(s_mm, s * UNITS + u + 1)
                nc.vector.tensor_reduce(nmx[:, h // HPC, half, h % HPC:h % HPC + 1],
                                        S[:, 2 * (u % 2):2 * (u % 2) + 2, :].rearrange("p n k -> p (n k)"),
                                        AX.X, ALU.max, negate=True).then_inc(nmx_made, 1)

            def factors_start(s):
                dve.wait_ge(exp_done, UNITS * (s + 1))
                nc.vector.tensor_tensor(nmin[:, :, :], nmx[:, :, 0, :], nmx[:, :, 1, :], ALU.min).then_inc(fac_step, 1)
                dve.wait_ge(fac_step, 5 * s + 1)
                nc.vector.tensor_tensor(fac[:, :, :, :], nmin[:, :, :].unsqueeze(2).to_broadcast([P, OC, 2, HPC]),
                                        nmx[:, :, :, :], ALU.subtract).then_inc(fac_step, 1)

            def factors_end(s):
                dve.wait_ge(fac_exp, s + 1)
                nc.vector.tensor_tensor(den[:, :, :, :], den[:, :, :, :], fac[:, :, :, :], ALU.mult).then_inc(fac_step, 1)
                dve.wait_ge(fac_step, 5 * s + 3)
                nc.vector.tensor_tensor(dsum[:, :, :], den[:, :, 0, :], den[:, :, 1, :], ALU.add).then_inc(fac_step, 1)
                dve.wait_ge(fac_step, 5 * s + 4)
                nc.vector.reciprocal(nmin[:, :, :], dsum[:, :, :]).then_inc(fac_step, 1)
                dve.wait_ge(fac_step, 5 * s + 5)
                dve.wait_ge(t_mm, s * STAGE_STEPS + (PAIRS - 1) * STEPS)
                for o in range(OC):
                    for i in range(2):
                        f = nc.vector.tensor_tensor(
                            fac_rep[:, 2 * o:2 * o + 2, i, :, :],
                            fac[:, o, i, :].rearrange("p (a l) -> p a l", l=2).unsqueeze(3).to_broadcast([P, 2, 2, 2 * HD]),
                            nmin[:, o, :].rearrange("p (a l) -> p a l", l=2).unsqueeze(3).to_broadcast([P, 2, 2, 2 * HD]),
                            ALU.mult)
                f.then_inc(fac_made, 1)

            def stage(s, last):
                for what, n in PROJ:
                    if what == "K":
                        dve.wait_ge(k_mm, s * NCH + n + 1)
                        part = [k_parts[n // 2 % 2][:, l, :, (n % 2) * CK:(n % 2 + 1) * CK] for l in range(2)]
                        if n % 2 == 0 and n >= 4:
                            for g in range(HPC):
                                dve.wait_ge(k_stacked[g][n // 2 % 2], KST * (s * (NCH // 4) + n // 4))
                        elif n == 0:
                            dve.wait_ge(t_mm, s * STAGE_STEPS)
                        for o in range(OC):
                            i = nc.vector.tensor_scalar(part[0][:, o].bitcast(F32R), TP[:, n % 2, o * CK:(o + 1) * CK],
                                                        bias_x[:, 1, bass.ds((s % 2) * OC + o, 1)], None, ALU.add)
                        i.then_inc(k_hi_out, 1)
                        dve.wait_ge(k_hi_out, s * NCH + n + 1)
                        for o in range(OC):
                            i = nc.vector.scalar_tensor_tensor(part[1][:, o].bitcast(F32R), TP[:, n % 2, o * CK:(o + 1) * CK],
                                                               bias_x[:, 1, bass.ds((s % 2) * OC + o, 1)],
                                                               part[0][:, o], ALU.add, ALU.subtract)
                        i.then_inc(k_out, 1)
                    elif what == "V":
                        dve.wait_ge(v_hi_out, s * NCH + n + 1)
                        src = TP[:, 2, :] if n % 2 == 0 else O[:, :]
                        nc.vector.tensor_tensor(v_pk[:, 2 * n:2 * n + 2, :, 1, :], src.rearrange("p (k h d) -> p k h d", k=2, h=HS),
                                                f32(v_pk[:, 2 * n:2 * n + 2, :, 0, :]), ALU.subtract).then_inc(v_out, 1)
                        if n + 2 < NCH:
                            split_c(s, n + 2)
                    elif what == "S":
                        maximum(s, n)
                    elif what == "fold":
                        folded_out(s)
                for g in range(STAGE_STEPS):
                    p, j = g // STEPS, g % STEPS
                    dve.wait_ge(pt_hi_out, s * STAGE_STEPS + g + 1)
                    nc.vector.tensor_tensor(pt_lo[:, g % PB, :], TP[:, g % TB, :], f32(pt_hi[:, g % PB, :]),
                                            ALU.subtract).then_inc(pt_out, 1)
                    if g in SCORES_AT:
                        maximum(s, SCORES_AT[g])
                    if g == FAC_AT:
                        factors_start(s)
                    if g == FAC_AT + 1:
                        factors_end(s)
                dve.wait_ge(rb_mm, s + 1)
                dve.wait_ge(o_out, (s + 1) * PAIRS)
                nc.vector.tensor_tensor(oraw[:, :, :, :].rearrange("p a i t -> p (a i t)"),
                                        S[:, 0:2, :].rearrange("p n k -> p (n k)"),
                                        oraw[:, :, :, :].rearrange("p a i t -> p (a i t)"), ALU.mult).then_inc(o_normed, 1)
                dve.wait_ge(o_normed, s + 1)
                nc.vector.tensor_tensor(oraw[:, :, 0, :], oraw[:, :, 0, :], oraw[:, :, 1, :], ALU.add).then_inc(o_summed, 1)

            def folded_out(s):
                if isinstance(s, int) and s == 0:
                    return
                half, b = (s + 1) % 2, (s - 1) // 2
                dve.wait_ge(fold_mm, s)
                for o in range(OC):
                    nc.vector.tensor_scalar(aT[:, bass.ds(half * OC + o, 1), bass.ds(b * T, T)],
                                            S[:, 2, o * T:(o + 1) * T].unsqueeze(1), bias_x[:, 2, bass.ds(half * OC + o, 1)],
                                            None, ALU.add).then_inc(a_done, 1)

            all_stages(dve, first, stage)
            folded_out(STAGES)

            dve.wait_ge(x1_in, 16)
            dve.wait_ge(row_in, 32)
            nc.vector.tensor_tensor(x1[:, :, :], x1[:, :, :], rb_x[:, :].unsqueeze(1).to_broadcast([P, B, D]), ALU.add).then_inc(bo_added, 1)
            dve.wait_ge(bo_added, 1)
            for b in range(B):
                dve.wait_ge(oproj_mm, b + 1)
                nc.vector.tensor_tensor(x1[:, b, :], S[:, oproj_bank(b), :], x1[:, b, :], ALU.add).then_inc(x1_done, 1)
                dve.wait_ge(x1_done, b + 1)
                layer_norm(1, b, x1, xn)
            for b in range(B):
                transposed_out(1, b, xnT)
            nc.vector.tensor_tensor(x1[:, :, :], x1[:, :, :], rb_a[:, :].unsqueeze(1).to_broadcast([P, B, D]), ALU.add).then_inc(bo2_added, 1)

            def split_e(e, slot, k):
                dve.wait_ge(e_hi_made, 3 * e + k + 1)
                nc.vector.tensor_tensor(e_lo(slot)[:, k], eraw[:, k], f32(e_hi(slot)[:, k]), ALU.subtract).then_inc(e_made, 1)

            split_e(0, 0, 0)
            for n in range(2):
                dve.wait_ge(sp_mm, 1 + n)
                for o in range(2):
                    oc = 2 * n + o
                    i = nc.vector.tensor_scalar(q_s[:, oc, :], S[:, n, o * TOK:(o + 1) * TOK],
                                                bias_a[:, 0, oc:oc + 1], SC, ALU.add, ALU.mult)
                i.then_inc(sq_out, 1)
            split_e(0, 0, 1)

            def self_v(b):
                if b == 0:
                    dve.wait_ge(rb_v_in, 16)
                dve.wait_ge(sp_mm, 5 + b)
                nc.vector.tensor_tensor(v_s[:, b, :], TP[:, b, :], rb_v[:, :], ALU.add).then_inc(sv_out, 1)

            def self_max(n):
                dve.wait_ge(ss_mm, n + 1)
                nc.vector.tensor_reduce(snmx[:, n, :], S[:, n % HPC, :].rearrange("p (c t) -> p c t", c=IC), AX.X,
                                        ALU.max, negate=True).then_inc(ss_max, 1)

            def self_rd(n):
                dve.wait_ge(ss_exp, n + 1)
                nc.vector.reciprocal(srd[:, n, :], ssum[:, n, :]).then_inc(ss_rd, 1)

            def self_pt(n):
                dve.wait_ge(sT_mm, n + 1)
                if n >= PTS:
                    dve.wait_ge(so_mm, n - PTS + 1)
                nc.vector.tensor_copy(pt_s[:, n % PTS].rearrange("p c t -> p (c t)"), TP[:, n % 2, :]).then_inc(sT_out, 1)
                if n % HPC == HPC - 1:
                    b = n // HPC
                    dve.wait_ge(so_mm, HPC * (b + 1))
                    nc.vector.tensor_copy(a2T[:, :, b * T:(b + 1) * T],
                                          (TP[:, 2, :] if b == 0 else O[:, :]).rearrange("p (c t) -> p c t", c=IC)).then_inc(so_out, 1)

            self_v(0)
            for n in range(B * HPC + 3):
                if n < B * HPC:
                    self_max(n)
                if n == 1:
                    split_e(0, 0, 2)
                if n == 3:
                    self_v(1)
                if 1 <= n <= B * HPC:
                    self_rd(n - 1)
                if n >= 3:
                    self_pt(n - 3)
            dve.wait_ge(bo2_added, 1)
            for b in range(B):
                dve.wait_ge(oproj2_mm, b + 1)
                nc.vector.tensor_tensor(x1[:, b, :], S[:, b, :], x1[:, b, :], ALU.add).then_inc(x2_done, 1)
                dve.wait_ge(x2_done, b + 1)
                layer_norm(2, b, x1, xn)
            for b in range(B):
                dve.wait_ge(x3_hi_made, b + 1)
                nc.vector.tensor_tensor(x3_lo[:, :, b * T:(b + 1) * T], TP[:, b, :].rearrange("p (c t) -> p c t", c=IC),
                                        f32(x3_hi[:, :, b * T:(b + 1) * T]), ALU.subtract).then_inc(x3_made, 1)
                transposed_out(2, b, xnT)
            split_e(1, 1, 0)

            steps = [0]

            def step(i):
                steps[0] += 1
                i.then_inc(gate_step, 1)
                dve.wait_ge(gate_step, steps[0])

            dve.wait_ge(gate_mm, 1)
            for b in range(B):
                i = nc.vector.tensor_reduce(gsm[:, b, 0:1], TP[:, 2, b * E:(b + 1) * E], AX.X, ALU.max, negate=True)
            step(i)
            dve.wait_ge(gate_exp, B)
            step(nc.vector.memset(sc16[:, :, E:2 * E], -1.0))
            step(nc.vector.reciprocal(gsm[:, :, 2], gsm[:, :, 1]))
            split_e(1, 1, 1)
            for b in range(B):
                step(nc.vector.tensor_scalar(sc16[:, b, 0:E], sc16[:, b, 0:E], gsm[:, b, 2:3], None, ALU.mult))
                step(nc.vector.max(top8[:, b, :], sc16[:, b, 0:E]))
                step(nc.vector.memset(top8[:, b, 2:8], -1.0))
                step(nc.vector.match_replace(rep16[:, b, :], top8[:, b, :], sc16[:, b, :], 0.0))
                step(nc.vector.tensor_tensor(comb[:, b, 0:E], sc16[:, b, 0:E], rep16[:, b, 0:E], ALU.subtract))
                step(nc.vector.memset(comb[:, b, E:NE], 1.0))
            assert steps[0] == GATE_STEPS

            def second_biases():
                dve.wait_ge(b2_mm, 1)
                for b in range(B):
                    nc.vector.tensor_tensor(x1[:, b, :], S[:, B + b, :], x1[:, b, :], ALU.add).then_inc(acc_step, 1)

            def add_expert(e, slot):
                for b in range(B):
                    dve.wait_ge(y_mm, B * e + b + 1)
                    dve.wait_ge(acc_step, B * (e + 1))
                    nc.vector.scalar_tensor_tensor(x1[:, b, :], S[:, 2 * slot + b, :], comb[:, b, bass.ds(e, 1)],
                                                   x1[:, b, :], ALU.mult, ALU.add).then_inc(acc_step, 1)

            def expert(e, slot, first_one, last_one):
                for f in range(FC):
                    if f == 3 and first_one:
                        dve.wait_ge(combT_mm, 1)
                        nc.vector.tensor_copy(combT[:, :], S[0:NE, 0, 0:TOK]).then_inc(combT_out, 1)
                    dve.wait_ge(silu_made, FC * e + f + 1)
                    nc.vector.scalar_tensor_tensor(gf[:, f % 2, :], up_bank(f)[:, TOK:2 * TOK], ebs[:, 1, bass.ds(e, 1), f],
                                                   silu[:, f % 2, :], ALU.add, ALU.mult).then_inc(g_made, 1)
                    dve.wait_ge(g_hi_made, FC * e + f + 1)
                    nc.vector.tensor_tensor(g_lo[:, slot, f, :], gf[:, f % 2, :], f32(g_hi[:, slot, f, :]),
                                            ALU.subtract).then_inc(g_split, 1)
                    if f == 2 and isinstance(e, int) and e == 1:
                        second_biases()
                    if f == 2 and not first_one:
                        add_expert(e - 1, 1 - slot)
                    if f < 3 and not last_one and not (first_one and f < 2):
                        split_e(e + 1, 1 - slot, f)
                if last_one:
                    add_expert(e, slot)

            all_experts(dve, expert)


def kernel(**inputs):
    import numpy as np
    import concourse.bacc as bacc
    from concourse.bass_utils import run_bass_kernel_spmd

    a = {k: np.asarray(v) for k, v in inputs.items()}

    def rows(w):
        s = w.shape
        return np.swapaxes(w.reshape(s[:-2] + (IC, P, s[-1])), -3, -2)

    def cols(v):
        return np.moveaxis(v.reshape(v.shape[:-1] + (IC, P)), -1, 0)

    def lin(names):
        return np.stack([rows(a[n].T) for n in names])

    ctxT = a["ctx_1024"].reshape(B, NCH, CK, IC, P).transpose(0, 1, 4, 3, 2)
    x, f, s = "L0_xattn_", "L0_ffn_", "L0_attn_"

    def experts(n, m):
        return np.concatenate([a[f + n], a[f + m][None]])

    data = {
        "x": a["x"], "ctxT": ctxT, "mask": a["mask_BxS2_bf0"],
        "xwT": lin([x + "wq", x + "wk", x + "wv", x + "wo"]),
        "xbias": cols(np.stack([a[x + "bq"], a[x + "bk"], a[x + "bv"]])),
        "awT": lin([s + "Wq", s + "Wk", s + "Wv", s + "Wo"]),
        "abias": cols(np.stack([a[s + "bq"], a[s + "bk"], a[s + "bv"]])),
        "rowbias": np.stack([a[x + "bo"], a[s + "bo"], a[s + "bv"]]),
        "gateT": rows(a[f + "gate_w"].T),
        "w1": rows(experts("w1", "sw1")), "w3": rows(experts("w3", "sw3")), "w2": rows(experts("w2", "sw2")),
        "eb": cols(np.stack([experts("b1", "sb1"), experts("b3", "sb3")])),
        "eb2": experts("b2", "sb2"),
    }
    nc = bacc.Bacc("TRN2", target_bir_lowering=False, num_devices=1)
    arrays, args = {}, []
    for name, v in data.items():
        v = np.ascontiguousarray(v)
        arrays[name] = v
        args.append(nc.dram_tensor(name, v.shape, mybir.dt.from_np(v.dtype), kind="ExternalInput").ap())
    args.append(nc.dram_tensor("out", (B, T, D), F32, kind="ExternalOutput").ap())
    perceiver_kernel(nc, *args)
    r = run_bass_kernel_spmd(nc, [arrays], core_ids=[0])
    return r.results[0]["out"]
```
